# Optimizing a Trainium2 kernel written in Bass

```python
import numpy as np
import jax
import jax.numpy as jnp

def _softmax(x, axis=-1):
    return jax.nn.softmax(x, axis=axis)

def _gelu(x):
    return jax.nn.gelu(x, approximate=True)

def _silu(x):
    return jax.nn.silu(x)

def _sigmoid(x):
    return jax.nn.sigmoid(x)

def _layernorm(x, axis=-1, eps=1e-05):
    m = jnp.mean(x, axis=axis, keepdims=True)
    v = jnp.var(x, axis=axis, keepdims=True)
    return (x - m) / jnp.sqrt(v + eps)

def _scatter_add(tgt, idx, src, axis=0):
    return tgt.at[idx].add(src)

def _segment_sum(src, seg, n):
    return jax.ops.segment_sum(src, seg, n)
kernel_name = 'mk_rec_standalone_d1_rec_r8_4a066f'

def setup_inputs(seed: int=0):
    np.random.seed(seed)
    _w = jnp.asarray

    def _rec_inputs():
        import jax
        import jax.numpy as jnp
        _rk = jax.random.key(seed)
        r_x = -0.000292821 + 1.00034 * jax.random.normal(jax.random.fold_in(_rk, 1), (2048, 1024), jnp.float32)
        r_user_indices = jax.random.randint(jax.random.fold_in(_rk, 2), (2048,), 1, 9999, jnp.int32)
        r_item_indices = jax.random.randint(jax.random.fold_in(_rk, 3), (2048,), 2, 9994, jnp.int32)
        return (r_x, r_user_indices, r_item_indices)
    r_x, r_user_indices, r_item_indices = _rec_inputs()

    def _L0_rec_setup():
        import jax, jax.numpy as jnp
        import numpy as np
        IN_F = 1024
        OUT_F = 1024
        R = 16
        NUM_USERS = 1250
        NUM_ITEMS = 1250
        BATCH = 512
        SCALING = 32.0 / 16.0
        key = jax.random.key(seed)
        ks = jax.random.split(key, 9)
        return {'x': jax.random.normal(ks[0], (BATCH, IN_F), dtype=jnp.float32), 'user_indices': jax.random.randint(ks[1], (BATCH,), 0, NUM_USERS, dtype=jnp.int32), 'item_indices': jax.random.randint(ks[2], (BATCH,), 0, NUM_ITEMS, dtype=jnp.int32), 'W_base': jax.random.normal(ks[3], (OUT_F, IN_F), dtype=jnp.float32) * 0.02, 'b_base': jax.random.normal(ks[4], (OUT_F,), dtype=jnp.float32) * 0.02, 'A': jax.random.normal(ks[5], (R, IN_F), dtype=jnp.float32) * 0.02, 'B_user': jax.random.normal(ks[6], (NUM_USERS, OUT_F, R), dtype=jnp.float32) * 0.02, 'B_item': jax.random.normal(ks[7], (NUM_ITEMS, OUT_F, R), dtype=jnp.float32) * 0.02, 'W_common': jax.random.normal(ks[8], (OUT_F, R), dtype=jnp.float32) * 0.02}
    _L0_rec_all = _L0_rec_setup()
    _L0_rec_in = {k: v for k, v in _L0_rec_all.items() if k in ('W_base', 'b_base', 'A', 'B_user', 'B_item', 'W_common')}
    del _L0_rec_all
    return {'r_x': r_x, 'r_user_indices': r_user_indices, 'r_item_indices': r_item_indices, 'L0_rec_W_base': _L0_rec_in['W_base'], 'L0_rec_b_base': _L0_rec_in['b_base'], 'L0_rec_A': _L0_rec_in['A'], 'L0_rec_B_user': _L0_rec_in['B_user'], 'L0_rec_B_item': _L0_rec_in['B_item'], 'L0_rec_W_common': _L0_rec_in['W_common']}

def reference(r_x, r_user_indices, r_item_indices, L0_rec_W_base, L0_rec_b_base, L0_rec_A, L0_rec_B_user, L0_rec_B_item, L0_rec_W_common):
    import jax
    import jax.numpy as jnp

    def _L0_rec_ref(x, user_indices, item_indices, W_base, b_base, A, B_user, B_item, W_common):
        import jax, jax.numpy as jnp
        import numpy as np
        IN_F = 1024
        OUT_F = 1024
        R = 16
        NUM_USERS = 1250
        NUM_ITEMS = 1250
        BATCH = 512
        SCALING = 32.0 / 16.0
        base = x @ W_base.T + b_base
        a = x @ A.T
        Bu = B_user[user_indices]
        Bi = B_item[item_indices]
        user_part = jnp.einsum('bor,br->bo', Bu, a)
        item_part = jnp.einsum('bor,br->bo', Bi, a)
        common_part = a @ W_common.T
        return base + SCALING * (user_part + item_part + common_part)
    y = _L0_rec_ref(r_x, r_user_indices, r_item_indices, L0_rec_W_base, L0_rec_b_base, L0_rec_A, L0_rec_B_user, L0_rec_B_item, L0_rec_W_common)
    return y

_drawn_inputs = setup_inputs


def setup_inputs(seed=0):
    import zlib

    import numpy as np

    out = dict(_drawn_inputs(seed))
    spreads = {}
    factors = {}
    for name, (base, spread) in spreads.items():
        noise = np.random.default_rng([zlib.crc32(name.encode()), seed]).standard_normal(out[name].shape)
        drawn = base * np.exp(spread * noise) if base else spread * noise
        out[name] = jnp.asarray(drawn.astype(out[name].dtype))
    for name, factor in factors.items():
        out[name] = (out[name] * factor).astype(out[name].dtype)
    return out
```

```python
from contextlib import ExitStack

import concourse.bass as bass
from concourse import mybir

P = 128
BATCH, IN_F, OUT_F, R = 2048, 1024, 1024, 16
ROWS = 1250
TABLES = 2
KC = IN_F // P
HALVES = OUT_F // 512
TILES = BATCH // P
GT = 3
GROUPS = -(-TILES // GT)
GS = GT * P
COLS = TILES * TABLES
GC = GT * TABLES
RB = 2
CHUNKS = R // RB
CHUNK = RB * OUT_F
SLOTS = 3
WSLOTS = 3
XH = KC // 2
ABSENT = float(1 << 16)
TABLE_CHUNKS = TABLES * ROWS * CHUNKS
NL = 3 * TABLES * R
NB = 2
NC = 3 * R
INFO = 2 + 2 * R


def tiles_of(g):
    return range(g * GT, min((g + 1) * GT, TILES))


def samples_of(g):
    return len(tiles_of(g)) * P


def rec_kernel(nc, idx, x_t, w_t, a_t, bias, common_t, table, out):
    f32, f32r, i32 = mybir.dt.float32, mybir.dt.float32r, mybir.dt.int32
    ALU, ACT, AX = mybir.AluOpType, mybir.ActivationFunctionType, mybir.AxisListType
    table_chunks = table.rearrange("n (c k) -> (n c) k", c=CHUNKS)

    ctx = ExitStack()
    with ctx:
        def sb(name, shape, dt=f32):
            return ctx.enter_context(nc.sbuf_tensor(name, shape, dt))

        def pb(name, shape):
            return ctx.enter_context(nc.psum_tensor(name, shape, f32))

        def sem(name):
            return ctx.enter_context(nc.semaphore(name))

        w_hi = sb("w_hi", [P, KC, OUT_F], f32r)
        w_lo = sb("w_lo", [P, KC, OUT_F], f32r)
        x_raw = sb("x_raw", [P, 2, XH * GS])
        x_hi = sb("x_hi", [P, 2, KC, GS], f32r)
        x_lo = sb("x_lo", [P, 2, KC, GS], f32r)
        a_raw = sb("a_raw", [P, KC, R])
        a_hl = sb("a_hl", [P, KC, 2 * R], f32r)
        last_w = sb("last_w", [NL + NB, OUT_F], f32r)
        common_w = sb("common_w", [NC, OUT_F], f32r)
        is_lo = sb("is_lo", [P, 2])
        lo_sign = sb("lo_sign", [P, 2])
        at_sb = sb("at_sb", [2 * R, GS])
        a_part = sb("a_part", [P, GT, R])
        a_all = sb("a_all", [P, TILES, R])
        a_hi = sb("a_hi", [P, GT, R], f32r)
        a_lo = sb("a_lo", [P, GT, R], f32r)
        low = sb("low", [P, GT, NL + NB + NC])
        last_t = sb("last_t", [NL + NB, 2, GS], f32r)
        common_a = sb("common_a", [NC, 2, GS], f32r)
        idx_i = sb("idx_i", [P, COLS], i32)
        row = sb("row", [P, COLS])
        wrap = sb("wrap", [P, COLS])
        in_mask = sb("in_mask", [P, GROUPS * GC])
        last_mask = sb("last_mask", [P, COLS])
        counts = sb("counts", [P, 2, GROUPS * GC])
        first = sb("first", [P, GROUPS, GC + 1])
        place = sb("place", [P, GROUPS * GC])
        info = sb("info", [P, TILES, TABLES, INFO], f32r)
        sample = sb("sample", [P, TILES])
        count_f = sb("count_f", [P, GS])
        below = sb("below", [P, P])
        ones = sb("ones", [P, P])
        ident = sb("ident", [P, P])
        onehot = sb("onehot", [P, GC, P], f32r)
        entry = sb("entry", [P, INFO])
        a_entry = sb("a_entry", [P, R])
        first_chunk = sb("first_chunk", [P, 1])
        chunk_no = sb("chunk_no", [P, CHUNKS])
        fetch = sb("fetch", [P, CHUNKS], i32)
        select = sb("select", [P, 2, GS], f32r)
        rows = sb("rows", [P, SLOTS, CHUNK])
        staging = sb("staging", [P, WSLOTS, OUT_F])
        out_sb = staging[:, 0:2, :]
        acc = staging[:, 2, :]
        acc_hi = sb("acc_hi", [P, OUT_F], f32r)
        acc_lo = sb("acc_lo", [P, OUT_F], f32r)
        longest = sb("longest", [P, 1])
        longest_i = sb("longest_i", [P, 1], i32)
        over = sb("over", [P, COLS])
        over_chunk = sb("over_chunk", [P, COLS])
        over_fetch_all = sb("over_fetch_all", [P, COLS, CHUNKS], i32)
        over_fetch = sb("over_fetch", [P, TABLES, CHUNKS], i32)
        over_a = sb("over_a", [P, TABLES, R])

        main_ps = [pb(f"main_ps{i}", [P, OUT_F]) for i in range(GT)]
        ps_a = pb("ps_a", [P, 512])
        ps_b = pb("ps_b", [P, 512])
        at_ps = ps_a[0:2 * R, 0:GS]
        common_ps = ps_a[0:NC, 0:GS]
        entry_ps = ps_a[:, GS:GS + INFO]
        a_ps = ps_b[:, 0:GT * 2 * R].rearrange("p (t r) -> p t r", r=2 * R)
        counts_ps = ps_b[:, 0:2 * COLS]
        last_ps = ps_b[0:NL + NB, P:P + GS]

        idx_loaded, a_loaded, last_loaded = sem("idx_loaded"), sem("a_loaded"), sem("last_loaded")
        common_loaded = sem("common_loaded")
        x_loaded = [sem(f"x_loaded{i}") for i in range(2)]
        w_loaded = [sem(f"w_loaded{i}") for i in range(WSLOTS)]
        gathered = [sem(f"gathered{i}") for i in range(SLOTS)]
        stored = [sem(f"stored{i}") for i in range(2)]
        consts_ready, masks_made = sem("consts_ready"), sem("masks_made")
        a_hi_done, x_hi_done, w_hi_done = sem("a_hi_done"), sem("x_hi_done"), sem("w_hi_done")
        at_copied, low_copied, shared_hi = sem("at_copied"), sem("low_copied"), sem("shared_hi")
        acc_hi_done, evacuated = sem("acc_hi_done"), sem("evacuated")
        dve_step = sem("dve_step")
        a_lo_done, x_lo_done, w_lo_done = sem("a_lo_done"), sem("x_lo_done"), sem("w_lo_done")
        in_mask_ready, counts_taken = sem("in_mask_ready"), sem("counts_taken")
        a_taken, low_ready, info_ready, onehot_ready = sem("a_taken"), sem("low_ready"), sem("info_ready"), sem("onehot_ready")
        entry_taken, fetch_ready, select_ready = sem("entry_taken"), sem("fetch_ready"), sem("select_ready")
        rows_used, acc_lo_done, shared_ready = sem("rows_used"), sem("acc_lo_done"), sem("shared_ready")
        longest_ready = sem("longest_ready")
        counts_done, at_done, a_done = sem("counts_done"), sem("at_done"), sem("a_done")
        entry_done, low_t_done, x_used, tile_done = sem("entry_done"), sem("low_t_done"), sem("x_used"), sem("tile_done")
        over_ready, over_gathered, over_used = sem("over_ready"), [sem(f"over_gathered{i}") for i in range(2)], sem("over_used")
        over_stored, over_cleared = sem("over_stored"), sem("over_cleared")

        def x_half(buf, g, half, k=None):
            return buf[:, g % 2, half * XH:(half + 1) * XH, 0:samples_of(g)]

        last_raw = staging[0:NL + NB, KC % WSLOTS, :]
        common_raw = staging[0:NC, (KC + 1) % WSLOTS, :]
        hi_tmp = acc_hi[0:NL + NB, :]

        def x_raw_half(g, half):
            n = samples_of(g)
            return x_raw[:, half, 0:XH * n].rearrange("p (k b) -> p k b", b=n)

        block = ctx.enter_context(nc.Block())

        @block.sync
        def _(sp):
            def load_x(g, half):
                if g >= 1:
                    sp.wait_ge(x_lo_done, 2 * (g - 1) + half + 1)
                n = samples_of(g)
                at = g * KC * GS + half * XH * n
                sp.dma_start(x_raw[:, half, 0:XH * n], x_t[:, at:at + XH * n]).then_inc(x_loaded[half], 16)

            def stage_free(n):
                if n >= WSLOTS:
                    sp.wait_ge(w_lo_done, n - WSLOTS + 1)

            def load_w(k):
                stage_free(k)
                sp.dma_start(staging[:, k % WSLOTS, :], w_t[:, k, :]).then_inc(w_loaded[k % WSLOTS], 16)

            sp.dma_start(idx_i[:, :], idx).then_inc(idx_loaded, 16)
            sp.dma_start(a_raw[:, :, :], a_t).then_inc(a_loaded, 16)
            load_x(0, 0)
            load_x(0, 1)
            for k in range(WSLOTS):
                load_w(k)
            for k in range(WSLOTS, KC):
                load_w(k)
            stage_free(KC)
            for part in range(3):
                for tab in range(TABLES):
                    at = (part * TABLES + tab) * R
                    sp.dma_start(last_raw[at:at + R, :],
                                 table[(tab + 1) * ROWS - 1, :].rearrange("(r o) -> r o", r=R)).then_inc(last_loaded, 16)
            for part in range(NB):
                sp.dma_start(last_raw[NL + part:NL + part + 1, :], bias).then_inc(last_loaded, 16)
            stage_free(KC + 1)
            for part in range(3):
                sp.dma_start(common_raw[part * R:(part + 1) * R, :], common_t).then_inc(common_loaded, 16)
            load_x(1, 0)
            load_x(1, 1)
            for t in range(TILES):
                if t % GT == 0 and t // GT + 2 < GROUPS:
                    load_x(t // GT + 2, 0)
                    load_x(t // GT + 2, 1)
                sp.wait_ge(evacuated, t + 1)
                sp.dma_start(out[t * P:(t + 1) * P, :], out_sb[:, t % 2, :]).then_inc(stored[t % 2], 16)
            for i in range(2):
                sp.wait_ge(stored[i], 16 * (TILES // 2))

        @block.gpsimd
        def _(pool):
            pool.memset(ones[:, :], 1.0).then_inc(masks_made, 1)
            pool.memset(in_mask[:, COLS:GROUPS * GC], 0.0).then_inc(consts_ready, 1)
            pool.memset(counts[:, :, :], 0.0).then_inc(consts_ready, 1)
            pool.memset(first[:, :, 0:1], 0.0).then_inc(consts_ready, 1)
            pool.memset(low[:, :, NL:NL + NB], 1.0).then_inc(consts_ready, 1)
            pool.iota(count_f[:, :], pattern=[[1, GS]], base=1, channel_multiplier=0,
                      allow_small_or_imprecise_dtypes=True).then_inc(consts_ready, 1)
            pool.iota(chunk_no[:, :], pattern=[[1, CHUNKS]], base=-CHUNKS, channel_multiplier=0,
                      allow_small_or_imprecise_dtypes=True).then_inc(consts_ready, 1)
            whole = TILES // GT * GT
            pool.iota(sample[:, 0:whole], pattern=[[0, whole // GT], [P, GT]], base=1, channel_multiplier=1,
                      allow_small_or_imprecise_dtypes=True).then_inc(consts_ready, 1)
            pool.iota(sample[:, whole:TILES], pattern=[[P, TILES - whole]], base=1, channel_multiplier=1,
                      allow_small_or_imprecise_dtypes=True).then_inc(consts_ready, 1)
            pool.wait_ge(masks_made, 1)
            pool.affine_select(out=below[:, :], in_=ones[:, :], compare_op=ALU.is_gt, fill=0.0, base=0,
                               pattern=[[1, P]], channel_multiplier=-1).then_inc(consts_ready, 1)
            pool.affine_select(out=ident[:, :], in_=ones[:, :], compare_op=ALU.is_equal, fill=0.0, base=0,
                               pattern=[[1, P]], channel_multiplier=-1).then_inc(consts_ready, 1)
            pool.memset(is_lo[:, :], 1.0).then_inc(masks_made, 1)
            pool.wait_ge(masks_made, 2)
            pool.affine_select(out=is_lo[:, 0:1], in_=is_lo[:, 0:1], compare_op=ALU.is_ge, fill=0.0,
                               base=-TABLES * R, pattern=[[0, 1]], channel_multiplier=1).then_inc(masks_made, 1)
            pool.affine_select(out=is_lo[:, 1:2], in_=is_lo[:, 1:2], compare_op=ALU.is_ge, fill=0.0,
                               base=-R, pattern=[[0, 1]], channel_multiplier=1).then_inc(masks_made, 1)
            pool.wait_ge(masks_made, 4)
            pool.affine_select(out=is_lo[:, 0:1], in_=is_lo[:, 0:1], compare_op=ALU.is_gt, fill=0.0,
                               base=2 * TABLES * R, pattern=[[0, 1]], channel_multiplier=-1).then_inc(masks_made, 1)
            pool.affine_select(out=is_lo[:, 1:2], in_=is_lo[:, 1:2], compare_op=ALU.is_gt, fill=0.0,
                               base=2 * R, pattern=[[0, 1]], channel_multiplier=-1).then_inc(consts_ready, 1)
            pool.wait_ge(masks_made, 5)
            pool.affine_select(out=is_lo[:, 0:1], in_=is_lo[:, 0:1], compare_op=ALU.not_equal, fill=1.0,
                               base=-(NL + 1), pattern=[[0, 1]], channel_multiplier=1).then_inc(consts_ready, 1)
            for s in range(SLOTS):
                pool.memset(rows[:, s, :], 0.0).then_inc(masks_made, 1)
            pool.wait_ge(masks_made, 5 + SLOTS)

            for g in range(GROUPS):
                pool.wait_ge(fetch_ready, g + 1)
                for c in range(CHUNKS):
                    n = g * CHUNKS + c
                    if n >= SLOTS:
                        pool.wait_ge(rows_used, n - SLOTS + 1)
                    pool.indirect_dma_start(
                        out=rows[:, n % SLOTS, :], out_offset=None, in_=table_chunks,
                        in_offset=bass.IndirectOffsetOnAxis(ap=fetch[:, c:c + 1], axis=0),
                        bounds_check=TABLE_CHUNKS - 1, oob_is_err=False).then_inc(gathered[n % SLOTS], 16)

            pool.wait_ge(longest_ready, 1)
            for i in range(2):
                pool.wait_ge(stored[i], 16 * (TILES // 2))
            last_chunk = pool.to_reg(TABLE_CHUNKS - 1)
            with pool.If(pool.value_load(longest_i[0:1, 0:1], min_val=0, max_val=GC * P) > P):
                with pool.Fori(0, TILES) as t:
                    pool.wait_ge(over_ready, t + 1)
                    pool.sem_inc(over_cleared, 1)
                    for n in range(TABLES * CHUNKS):
                        if n >= 2:
                            pool.wait_ge(over_used, t * (TABLES * CHUNKS) + n - 1)
                            pool.sem_inc(over_cleared, 1)
                        pool.indirect_dma_start(
                            out=rows[:, n % 2, :], out_offset=None, in_=table_chunks,
                            in_offset=bass.IndirectOffsetOnAxis(
                                ap=over_fetch[:, n // CHUNKS, n % CHUNKS:n % CHUNKS + 1], axis=0),
                            bounds_check=last_chunk, oob_is_err=False).then_inc(over_gathered[n % 2], 16)
                    pool.wait_ge(over_used, (t + 1) * (TABLES * CHUNKS))
                    pool.sem_inc(over_cleared, 1)
                    pool.dma_start(out[bass.ds(t * P, P), :], acc, accum_op=ALU.add).then_inc(over_stored, 16)
                    pool.wait_ge(over_stored, t * 16 + 16)

        @block.scalar
        def _(act):
            def split_x(g, half):
                act.wait_ge(x_loaded[half], 16 * (g + 1))
                if g >= 2:
                    act.wait_ge(x_used, g - 1)
                act.activation(x_half(x_hi, g, half), x_raw_half(g, half), ACT.Copy).then_inc(x_hi_done, 1)

            def split_w(k):
                act.wait_ge(w_loaded[k % WSLOTS], 16 * (k // WSLOTS + 1))
                act.activation(w_hi[:, k, :], staging[:, k % WSLOTS, :], ACT.Copy).then_inc(w_hi_done, 1)

            def copy_at(g):
                act.wait_ge(at_done, g + 1)
                if g >= 1:
                    act.wait_ge(a_done, g)
                n = samples_of(g)
                act.activation(at_sb[:, 0:n], at_ps[:, 0:n], ACT.Copy).then_inc(at_copied, 1)

            def copy_low(g):
                act.wait_ge(low_t_done, g + 1)
                if g >= 2:
                    act.wait_ge(tile_done, GT * (g - 1))
                n = samples_of(g)
                act.activation(last_t[:, g % 2, 0:n], last_ps[:, 0:n], ACT.Copy).then_inc(low_copied, 1)
                act.activation(common_a[:, g % 2, 0:n], common_ps[:, 0:n], ACT.Copy).then_inc(low_copied, 1)

            def split_acc(g):
                act.wait_ge(rows_used, CHUNKS * (g + 1))
                if g >= 1:
                    act.wait_ge(tile_done, GT * g)
                act.activation(acc_hi[:, :], acc, ACT.Copy).then_inc(acc_hi_done, 1)

            def evacuate(t):
                act.wait_ge(tile_done, t + 1)
                if t >= 2:
                    act.wait_ge(stored[t % 2], 16 * (t // 2))
                act.activation(out_sb[:, t % 2, :], main_ps[t % GT][:, :], ACT.Copy).then_inc(evacuated, 1)

            act.wait_ge(a_loaded, 16)
            act.activation(a_hl[:, :, 0:R], a_raw[:, :, :], ACT.Copy, scale=2.0).then_inc(a_hi_done, 1)
            split_x(0, 0)
            split_x(0, 1)
            split_w(0)
            copy_at(0)
            split_w(1)
            split_w(2)
            split_w(3)
            copy_low(0)
            for k in range(4, KC):
                split_w(k)
            act.wait_ge(last_loaded, 16 * (3 * TABLES + NB))
            act.activation(hi_tmp, last_raw, ACT.Copy).then_inc(shared_hi, 1)
            act.wait_ge(shared_ready, 1)
            act.wait_ge(common_loaded, 16 * 3)
            act.activation(hi_tmp[0:NC, :], common_raw, ACT.Copy).then_inc(shared_hi, 1)
            split_x(1, 0)
            split_x(1, 1)
            copy_at(1)
            split_acc(0)
            for t in tiles_of(0):
                evacuate(t)
            copy_low(1)
            split_x(2, 0)
            split_x(2, 1)
            copy_at(2)
            split_acc(1)
            evacuate(GT)
            evacuate(GT + 1)
            copy_low(2)
            for g in range(2, GROUPS):
                t = g * GT
                if g + 1 < GROUPS:
                    split_x(g + 1, 0)
                    split_x(g + 1, 1)
                evacuate(t - 1)
                if g + 1 < GROUPS:
                    copy_at(g + 1)
                split_acc(g)
                evacuate(t)
                if g + 1 < GROUPS:
                    copy_low(g + 1)
                    evacuate(t + 1)

        @block.vector
        def _(dve):
            steps = [0]

            def link(ins):
                steps[0] += 1
                ins.then_inc(dve_step, 1)
                dve.wait_ge(dve_step, steps[0])

            def split_x(g, half):
                dve.wait_ge(x_hi_done, 2 * g + half + 1)
                dve.tensor_tensor(x_half(x_lo, g, half), x_raw_half(g, half), x_half(x_hi, g, half).bitcast(f32),
                                  ALU.subtract).then_inc(x_lo_done, 1)

            def split_w(k):
                dve.wait_ge(w_hi_done, k + 1)
                dve.tensor_tensor(w_lo[:, k, :], staging[:, k % WSLOTS, :], w_hi[:, k, :].bitcast(f32),
                                  ALU.subtract).then_inc(w_lo_done, 1)

            def take_a(g):
                ts, n = tiles_of(g), len(tiles_of(g))
                t0, t1 = ts[0], ts[-1] + 1
                dve.wait_ge(a_done, g + 1)
                link(dve.tensor_copy(a_part[:, 0:n, :], a_ps[:, 0:n, 0:R]))
                dve.tensor_tensor(a_all[:, t0:t1, :], a_part[:, 0:n, :], a_ps[:, 0:n, R:2 * R],
                                  ALU.add).then_inc(a_taken, 1)
                dve.wait_ge(a_taken, g + 1)
                link(dve.tensor_copy(a_hi[:, 0:n, :], a_all[:, t0:t1, :]))
                link(dve.tensor_tensor(a_lo[:, 0:n, :], a_all[:, t0:t1, :], a_hi[:, 0:n, :].bitcast(f32), ALU.subtract))
                both = [P, n, TABLES, R]
                hi2 = a_hi[:, 0:n, :].bitcast(f32).unsqueeze(2).broadcast_to(both)
                lo2 = a_lo[:, 0:n, :].bitcast(f32).unsqueeze(2).broadcast_to(both)
                link(dve.tensor_copy(info[:, t0:t1, :, 2:2 + R], hi2))
                dve.tensor_copy(info[:, t0:t1, :, 2 + R:INFO], lo2).then_inc(info_ready, 1)
                if g >= 1:
                    dve.wait_ge(low_t_done, g)
                mask = last_mask[:, t0 * TABLES:t1 * TABLES].rearrange("p (t u) -> p t u", u=TABLES)
                mask = mask.unsqueeze(3).broadcast_to(both)
                for part, a2, a1 in ((0, hi2, a_hi), (1, hi2, a_hi), (2, lo2, a_lo)):
                    masked = low[:, 0:n, part * TABLES * R:(part + 1) * TABLES * R]
                    link(dve.tensor_tensor(masked.rearrange("p t (u r) -> p t u r", u=TABLES), a2, mask, ALU.mult))
                    at = NL + NB + part * R
                    common = dve.tensor_copy(low[:, 0:n, at:at + R], a1[:, 0:n, :].bitcast(f32))
                    if part < 2:
                        link(common)
                common.then_inc(low_ready, 1)

            def make_onehot(g):
                if g >= 1:
                    dve.wait_ge(entry_done, g)
                n = len(tiles_of(g)) * TABLES
                dve.tensor_tensor(onehot[:, 0:n, :], count_f[:, 0:P].unsqueeze(1).broadcast_to([P, n, P]),
                                  place[:, g * GC:g * GC + n].unsqueeze(2).broadcast_to([P, n, P]),
                                  ALU.is_equal).then_inc(onehot_ready, 1)

            def take_entries(g):
                dve.wait_ge(entry_done, g + 1)
                dve.tensor_copy(entry[:, :], entry_ps).then_inc(entry_taken, 1)
                dve.wait_ge(entry_taken, g + 1)
                link(dve.tensor_scalar(first_chunk[:, :], entry[:, 1:2], 0.0, ABSENT, ALU.is_equal, ALU.mult))
                link(dve.tensor_scalar(first_chunk[:, :], first_chunk[:, :], entry[:, 1:2], float(CHUNKS),
                                       ALU.add, ALU.mult))
                dve.tensor_scalar(fetch[:, :], chunk_no[:, :], first_chunk[:, 0:1], None, ALU.add).then_inc(fetch_ready, 1)
                link(dve.tensor_tensor(a_entry[:, :], entry[:, 2:2 + R], entry[:, 2 + R:INFO], ALU.add))
                if g >= 2:
                    dve.wait_ge(tile_done, GT * (g - 1))
                n = samples_of(g)
                dve.tensor_scalar(select[:, g % 2, 0:n], count_f[:, 0:n], entry[:, 0:1], None,
                                  ALU.is_equal).then_inc(select_ready, 1)

            def multiply_rows(buf, a_of, r, first_of_sum):
                if first_of_sum:
                    return dve.tensor_scalar(acc, buf, a_of(r), None, ALU.mult)
                return dve.scalar_tensor_tensor(acc, buf, a_of(r), acc, ALU.mult, ALU.add)

            def row_products(g):
                for c in range(CHUNKS):
                    n = g * CHUNKS + c
                    dve.wait_ge(gathered[n % SLOTS], 16 * (n // SLOTS + 1))
                    for j in range(RB):
                        r = c * RB + j
                        ins = multiply_rows(rows[:, n % SLOTS, j * OUT_F:(j + 1) * OUT_F],
                                            lambda r: a_entry[:, r:r + 1], r, r == 0)
                        if j < RB - 1:
                            link(ins)
                    ins.then_inc(rows_used, 1)
                    dve.wait_ge(rows_used, n + 1)
                    if g + 1 < GROUPS and g >= 1 and c in (3, 5):
                        split_x(g + 1, (c - 3) // 2)
                if g >= 1:
                    dve.wait_ge(tile_done, GT * g)
                dve.wait_ge(acc_hi_done, g + 1)
                dve.tensor_tensor(acc_lo[:, :], acc, acc_hi[:, :].bitcast(f32),
                                  ALU.subtract).then_inc(acc_lo_done, 1)
                dve.wait_ge(acc_lo_done, g + 1)

            dve.wait_ge(a_hi_done, 1)
            dve.scalar_tensor_tensor(a_hl[:, :, R:2 * R], a_raw[:, :, :], 2.0, a_hl[:, :, 0:R].bitcast(f32),
                                     ALU.mult, ALU.subtract).then_inc(a_lo_done, 1)
            dve.wait_ge(idx_loaded, 16)
            link(dve.tensor_copy(row[:, :], idx_i[:, :]))
            link(dve.tensor_scalar(wrap[:, :], row[:, :], 0.0, float(ROWS), ALU.is_lt, ALU.mult))
            link(dve.tensor_tensor(row[:, :], row[:, :], wrap[:, :], ALU.add))
            link(dve.tensor_scalar(row[:, :], row[:, :], 0.0, float(ROWS - 1), ALU.max, ALU.min))
            dve.wait_ge(consts_ready, 12)
            dve.tensor_scalar(in_mask[:, 0:COLS], row[:, :], float(ROWS - 1), None, ALU.is_lt).then_inc(in_mask_ready, 1)
            link(dve.tensor_scalar(last_mask[:, :], row[:, :], float(ROWS - 1), None, ALU.is_ge))
            row_v = row[:, :].rearrange("p (t u) -> p t u", u=TABLES)
            for tab in range(TABLES):
                link(dve.tensor_scalar(row_v[:, :, tab], row_v[:, :, tab], float(tab * ROWS + 1), None, ALU.add))
                link(dve.tensor_copy(info[:, :, tab, 0], sample[:, :]))
            link(dve.tensor_copy(info[:, :, :, 1], row_v))
            split_x(0, 0)
            split_x(0, 1)
            split_w(0)
            split_w(1)
            dve.wait_ge(counts_done, 1)
            dve.tensor_copy(counts[:, :, 0:COLS], counts_ps.rearrange("p (s c) -> p s c", s=2)).then_inc(counts_taken, 1)
            dve.wait_ge(counts_taken, 1)
            total = counts[:, 1, :].rearrange("p (g j) -> p g j", j=GC)
            for j in range(GC):
                link(dve.tensor_tensor(first[:, :, j + 1], first[:, :, j], total[:, :, j], ALU.add))
            place_v = place[:, :].rearrange("p (g j) -> p g j", j=GC)
            link(dve.tensor_tensor(place_v, counts[:, 0, :].rearrange("p (g j) -> p g j", j=GC),
                                   first[:, :, 0:GC], ALU.add))
            link(dve.scalar_tensor_tensor(place[:, :], place[:, :], 1.0, in_mask[:, :], ALU.add, ALU.mult))
            make_onehot(0)
            take_a(0)
            split_w(2)
            take_entries(0)
            for k in range(3, KC):
                split_w(k)
            link(dve.tensor_scalar(lo_sign[:, :], is_lo[:, :], -2.0, 1.0, ALU.mult, ALU.add))
            for i, (raw, to, n) in enumerate(((last_raw, last_w, NL + NB), (common_raw, common_w, NC))):
                dve.wait_ge(shared_hi, i + 1)
                link(dve.tensor_scalar(raw, raw, is_lo[0:n, i:i + 1], None, ALU.mult))
                dve.scalar_tensor_tensor(to[:, :], hi_tmp[0:n, :].bitcast(f32), lo_sign[0:n, i:i + 1], raw,
                                         ALU.mult, ALU.add).then_inc(shared_ready, 1)
            split_x(1, 0)
            split_x(1, 1)
            row_products(0)
            for g in range(1, GROUPS):
                take_a(g)
                make_onehot(g)
                take_entries(g)
                row_products(g)

            link(dve.tensor_reduce(longest[:, :], first[:, :, GC], axis=AX.X, op=ALU.max))
            dve.tensor_copy(longest_i[:, :], longest[:, :]).then_inc(longest_ready, 1)
            dve.wait_ge(longest_ready, 1)
            with dve.If(dve.value_load(longest_i[0:1, 0:1], min_val=0, max_val=GC * P) > P):
                link(dve.tensor_scalar(over[:, :], place[:, 0:COLS], float(P), None, ALU.is_gt))
                link(dve.tensor_scalar(over_chunk[:, :], over[:, :], -ABSENT, ABSENT, ALU.mult, ALU.add))
                link(dve.tensor_tensor(over_chunk[:, :], over_chunk[:, :], row[:, :], ALU.add))
                link(dve.tensor_scalar(over_chunk[:, :], over_chunk[:, :], float(CHUNKS), None, ALU.mult))
                link(dve.tensor_tensor(over_fetch_all[:, :, :], over_chunk[:, :].unsqueeze(2).broadcast_to([P, COLS, CHUNKS]),
                                       chunk_no[:, :].unsqueeze(1).broadcast_to([P, COLS, CHUNKS]), ALU.add))
                with dve.Fori(0, TILES) as t:
                    base = steps[0]
                    per_tile = TABLES + TABLES * R - TABLES * CHUNKS

                    def turn_link(ins, n):
                        ins.then_inc(dve_step, 1)
                        dve.wait_ge(dve_step, t * per_tile + (base + n))

                    dve.wait_ge(over_stored, t * 16)
                    for tab in range(TABLES):
                        turn_link(dve.tensor_scalar(over_a[:, tab, :], a_all[:, bass.ds(t, 1), :].squeeze(1),
                                                    over[:, bass.ds(t * TABLES + tab, 1)], None, ALU.mult), tab + 1)
                    dve.tensor_copy(over_fetch[:, :, :], over_fetch_all[:, bass.ds(t * TABLES, TABLES), :]).then_inc(over_ready, 1)
                    links = TABLES
                    for n in range(TABLES * CHUNKS):
                        tab, c = divmod(n, CHUNKS)
                        dve.wait_ge(over_gathered[n % 2], t * (16 * TABLES * CHUNKS // 2) + 16 * (n // 2 + 1))
                        for j in range(RB):
                            r = c * RB + j
                            ins = multiply_rows(rows[:, n % 2, j * OUT_F:(j + 1) * OUT_F],
                                                lambda r: over_a[:, tab, r:r + 1], r, n == 0 and j == 0)
                            if j < RB - 1:
                                links += 1
                                turn_link(ins, links)
                        ins.then_inc(over_used, 1)
                        dve.wait_ge(over_used, t * (TABLES * CHUNKS) + n + 1)

        @block.tensor
        def _(pe):
            def rank_a(g):
                pe.wait_ge(x_lo_done, 2 * g + 2)
                if g >= 1:
                    pe.wait_ge(low_copied, 2 * g)
                n = samples_of(g)
                for k in range(KC):
                    pe.matmul(at_ps[:, 0:n], a_hl[:, k, :], x_hi[:, g % 2, k, 0:n], start=(k == 0), stop=False)
                    last = pe.matmul(at_ps[0:R, 0:n], a_hl[:, k, 0:R], x_lo[:, g % 2, k, 0:n], start=False,
                                     stop=(k == KC - 1))
                last.then_inc(at_done, 1)

            def transpose_a(g):
                pe.wait_ge(at_copied, g + 1)
                if g >= 1:
                    pe.wait_ge(low_copied, 2 * g)
                else:
                    pe.wait_ge(counts_taken, 1)
                for j in range(len(tiles_of(g))):
                    last = pe.transpose(a_ps[:, j, :], at_sb[:, j * P:(j + 1) * P], ident[0:2 * R, 0:2 * R])
                last.then_inc(a_done, 1)

            def pack_entries(g):
                pe.wait_ge(onehot_ready, g + 1)
                pe.wait_ge(info_ready, g + 1)
                pe.wait_ge(at_copied, g + 1)
                cols = [(t, tab) for t in tiles_of(g) for tab in range(TABLES)]
                for c, (t, tab) in enumerate(cols):
                    last = pe.matmul(entry_ps, onehot[:, c, :], info[:, t, tab, :], start=(c == 0),
                                     stop=(c == len(cols) - 1))
                last.then_inc(entry_done, 1)

            def transpose_low(g):
                pe.wait_ge(low_ready, g + 1)
                pe.wait_ge(entry_taken, g + 1)
                for j in range(len(tiles_of(g))):
                    to = slice(j * P, (j + 1) * P)
                    pe.transpose(last_ps[:, to], low[:, j, 0:NL + NB], ident[:, :])
                    last = pe.transpose(common_ps[:, to], low[:, j, NL + NB:], ident[:, :])
                last.then_inc(low_t_done, 1)

            def base_step(t, half, k, start):
                g, j = divmod(t, GT)
                to = main_ps[t % GT][:, half * 512:(half + 1) * 512]
                b, o = slice(j * P, (j + 1) * P), slice(half * 512, (half + 1) * 512)
                pe.matmul(to, x_hi[:, g % 2, k, b], w_hi[:, k, o], start=start, stop=False)
                pe.matmul(to, x_hi[:, g % 2, k, b], w_lo[:, k, o], start=False, stop=False)
                return pe.matmul(to, x_lo[:, g % 2, k, b], w_hi[:, k, o], start=False, stop=False)

            def base(t, half):
                g = t // GT
                pe.wait_ge(x_lo_done, 2 * g + 2)
                pe.wait_ge(evacuated, t - GT + 1)
                for k in range(KC):
                    last = base_step(t, half, k, k == 0)
                if half == HALVES - 1 and t == tiles_of(g)[-1]:
                    last.then_inc(x_used, 1)

            def finish(t):
                g, j = divmod(t, GT)
                pe.wait_ge(shared_ready, 2)
                pe.wait_ge(low_copied, 2 * (g + 1))
                pe.wait_ge(select_ready, g + 1)
                b = slice(j * P, (j + 1) * P)
                for half in range(HALVES):
                    to = main_ps[t % GT][:, half * 512:(half + 1) * 512]
                    o = slice(half * 512, (half + 1) * 512)
                    pe.matmul(to, last_t[:, g % 2, b], last_w[:, o], start=False, stop=False)
                    pe.matmul(to, common_a[:, g % 2, b], common_w[:, o], start=False, stop=False)
                pe.wait_ge(acc_lo_done, g + 1)
                for half in range(HALVES):
                    to = main_ps[t % GT][:, half * 512:(half + 1) * 512]
                    o = slice(half * 512, (half + 1) * 512)
                    pe.matmul(to, select[:, g % 2, b], acc_hi[:, o], start=False, stop=False)
                    last = pe.matmul(to, select[:, g % 2, b], acc_lo[:, o], start=False, stop=True)
                last.then_inc(tile_done, 1)

            pe.wait_ge(consts_ready, 12)
            pe.wait_ge(masks_made, 1)
            pe.wait_ge(in_mask_ready, 1)
            pe.matmul(counts_ps[:, 0:COLS], below[:, :], in_mask[:, 0:COLS], start=True, stop=True)
            pe.matmul(counts_ps[:, COLS:2 * COLS], ones[:, :], in_mask[:, 0:COLS], start=True, stop=True).then_inc(counts_done, 1)
            pe.wait_ge(a_lo_done, 1)
            rank_a(0)
            for k in range(KC):
                pe.wait_ge(w_lo_done, k + 1)
                for t in tiles_of(0):
                    for half in range(HALVES):
                        last = base_step(t, half, k, k == 0)
                if k == KC - 1:
                    last.then_inc(x_used, 1)
                if k == 0:
                    transpose_a(0)
                elif k == 1:
                    pack_entries(0)
                elif k == 2:
                    transpose_low(0)
                elif k == KC - 2:
                    rank_a(1)
            finish(0)
            transpose_a(1)
            base(3, 0)
            finish(1)
            pack_entries(1)
            base(3, 1)
            finish(2)
            transpose_low(1)
            base(4, 0)
            base(4, 1)
            rank_a(2)
            finish(3)
            transpose_a(2)
            base(5, 0)
            pack_entries(2)
            base(5, 1)
            finish(4)
            transpose_low(2)
            for g in range(2, GROUPS):
                t, more = g * GT, g + 1 < GROUPS
                base(t, 0)
                base(t, 1)
                finish(t - 1)
                if more:
                    rank_a(g + 1)
                    base(t + 1, 0)
                    transpose_a(g + 1)
                    base(t + 1, 1)
                finish(t)
                if more:
                    pack_entries(g + 1)
                    base(t + 2, 0)
                    transpose_low(g + 1)
                    base(t + 2, 1)
                    finish(t + 1)


def kernel(**inputs):
    import numpy as np
    import concourse.bacc as bacc
    from concourse.bass_utils import run_bass_kernel_spmd

    a = {k: np.asarray(v) for k, v in inputs.items()}
    idx = np.stack([a["r_user_indices"].reshape(TILES, P), a["r_item_indices"].reshape(TILES, P)], axis=-1)
    x = a["r_x"].reshape(BATCH, KC, P).transpose(2, 1, 0)
    x_t = np.concatenate([x[:, :, g * GS:g * GS + samples_of(g)].reshape(P, -1) for g in range(GROUPS)], axis=1)
    tables = np.concatenate([a["L0_rec_B_user"], a["L0_rec_B_item"]], axis=0).transpose(0, 2, 1)
    arrays = {
        "idx": idx.transpose(1, 0, 2).reshape(P, COLS),
        "x_t": x_t,
        "w_t": a["L0_rec_W_base"].reshape(OUT_F, KC, P).transpose(2, 1, 0),
        "a_t": a["L0_rec_A"].reshape(R, KC, P).transpose(2, 1, 0),
        "bias": a["L0_rec_b_base"].reshape(1, OUT_F),
        "common_t": a["L0_rec_W_common"].T,
        "table": tables.reshape(TABLES * ROWS, R * OUT_F),
    }
    arrays = {k: np.ascontiguousarray(v) for k, v in arrays.items()}
    nc = bacc.Bacc("TRN2", target_bir_lowering=False, num_devices=1)
    args = [nc.dram_tensor(k, v.shape, mybir.dt.from_np(v.dtype), kind="ExternalInput").ap() for k, v in arrays.items()]
    args.append(nc.dram_tensor("out", (BATCH, OUT_F), mybir.dt.float32, kind="ExternalOutput").ap())
    rec_kernel(nc, *args)
    return run_bass_kernel_spmd(nc, [arrays], core_ids=[0]).results[0]["out"]
```

```python
from contextlib import ExitStack

import concourse.bass as bass
from concourse import mybir

P = 128
BATCH, IN_F, OUT_F, R = 2048, 1024, 1024, 16
ROWS = 1250
TABLES = 2
KC = IN_F // P
BANK = 512
HALVES = OUT_F // BANK
TILES = BATCH // P
GT = 3
GROUPS = -(-TILES // GT)
GS = GT * P
COLS = TILES * TABLES
GC = GT * TABLES
RB = 2
CHUNKS = R // RB
CHUNK = RB * OUT_F
SLOTS = 3
WSLOTS = 3
XH = KC // 2
ABSENT = float(1 << 16)
TABLE_CHUNKS = TABLES * ROWS * CHUNKS
INFO = 2 + 2 * R
LO = 64
NL = LO + TABLES * R
NC = LO + R + 1
CH = 2 * R + 1


def tiles_of(g):
    return range(g * GT, min((g + 1) * GT, TILES))


def samples_of(g):
    return len(tiles_of(g)) * P


def rec_kernel(nc, idx, x_t, w_t, a_t, bias, common_t, table, out):
    f32, f32r, i32 = mybir.dt.float32, mybir.dt.float32r, mybir.dt.int32
    ALU, ACT, AX = mybir.AluOpType, mybir.ActivationFunctionType, mybir.AxisListType
    table_chunks = table.rearrange("n (c k) -> (n c) k", c=CHUNKS)

    ctx = ExitStack()
    with ctx:
        def sb(name, shape, dt=f32):
            return ctx.enter_context(nc.sbuf_tensor(name, shape, dt))

        def pb(name, shape):
            return ctx.enter_context(nc.psum_tensor(name, shape, f32))

        def sem(name):
            return ctx.enter_context(nc.semaphore(name))

        w_hi = sb("w_hi", [P, KC, OUT_F], f32r)
        w_lo = sb("w_lo", [P, KC, OUT_F], f32r)
        x_raw = sb("x_raw", [P, 2, XH * GS])
        x_hi = sb("x_hi", [P, 2, KC, GS], f32r)
        x_lo = sb("x_lo", [P, 2, KC, GS], f32r)
        a_raw = sb("a_raw", [P, KC, R])
        a_hl = sb("a_hl", [P, KC, 2 * R], f32r)
        last_w = sb("last_w", [NL, OUT_F], f32r)
        common_w = sb("common_w", [NC, OUT_F], f32r)
        at_sb = sb("at_sb", [2 * R, GS])
        a_part = sb("a_part", [P, GT, R])
        a_all = sb("a_all", [P, TILES, R])
        a_split = sb("a_split", [P, GT, 2, R])
        low = sb("low", [P, GT, NL + NC])
        last_t = sb("last_t", [NL, 2, GS], f32r)
        common_a = sb("common_a", [NC, 2, GS], f32r)
        idx_i = sb("idx_i", [P, COLS], i32)
        row = sb("row", [P, COLS])
        wrap = sb("wrap", [P, COLS])
        in_mask = sb("in_mask", [P, GROUPS * GC])
        last_mask = sb("last_mask", [P, COLS])
        counts = sb("counts", [P, 2, GROUPS * GC])
        first = sb("first", [P, GROUPS, GC + 1])
        place = sb("place", [P, GROUPS * GC])
        info = sb("info", [P, TILES, TABLES, INFO], f32r)
        sample = sb("sample", [P, TILES])
        count_f = sb("count_f", [P, GS])
        ident = sb("ident", [P, P])
        onehot = sb("onehot", [P, GC, P], f32r)
        entry_row = sb("entry_row", [P, 2])
        entry_sample = sb("entry_sample", [P, GROUPS])
        entry_a = sb("entry_a", [P, 2 * R])
        a_entry = sb("a_entry", [P, R])
        first_chunk = sb("first_chunk", [P, 1])
        chunk_no = sb("chunk_no", [P, CHUNKS])
        fetch = sb("fetch", [P, 2, CHUNKS], i32)
        select = sb("select", [P, 2, GS], f32r)
        rows = sb("rows", [P, SLOTS, CHUNK])
        staging = sb("staging", [P, WSLOTS, OUT_F])
        out_sb = staging[:, 0:2, :]
        acc_sb = sb("acc", [P, OUT_F])
        acc = acc_sb[:, :]
        ones, below = acc_sb[:, 0:P], acc_sb[:, P:2 * P]
        last_raw = staging[0:NL, KC % WSLOTS, :]
        common_raw = staging[0:NC, (KC + 1) % WSLOTS, :]
        acc_hi = sb("acc_hi", [P, OUT_F], f32r)
        acc_lo = sb("acc_lo", [P, OUT_F], f32r)
        longest = sb("longest", [P, 1])
        longest_i = sb("longest_i", [P, 1], i32)
        over = sb("over", [P, COLS])
        over_chunk = sb("over_chunk", [P, COLS])
        over_fetch_all = x_raw[:, 0, 0:COLS * CHUNKS].bitcast(i32).rearrange("p (c k) -> p c k", k=CHUNKS)
        over_fetch = sb("over_fetch", [P, TABLES, CHUNKS], i32)
        over_a = sb("over_a", [P, TABLES, R])

        main_ps = [pb(f"main_ps{i}", [P, OUT_F]) for i in range(GT)]
        ps_a = pb("ps_a", [P, BANK])
        ps_b = pb("ps_b", [P, BANK])
        at_ps = ps_a[0:2 * R, 0:GS]
        common_ps = ps_a[0:NC, 0:GS]
        entry_row_ps = ps_a[:, GS:GS + 2]
        entry_a_ps = ps_a[:, GS:GS + 2 * R]
        a_ps = ps_b[:, 0:GT * 2 * R].rearrange("p (t r) -> p t r", r=2 * R)
        counts_ps = ps_b[:, 0:2 * COLS]
        last_ps = ps_b[0:NL, P:P + GS]

        idx_loaded, a_loaded = sem("idx_loaded"), sem("a_loaded")
        last_loaded, common_loaded = sem("last_loaded"), sem("common_loaded")
        x_loaded = [sem(f"x_loaded{i}") for i in range(2)]
        w_loaded = [sem(f"w_loaded{i}") for i in range(WSLOTS)]
        gathered = [sem(f"gathered{i}") for i in range(SLOTS)]
        stored = [sem(f"stored{i}") for i in range(2)]
        consts_ready, ones_made = sem("consts_ready"), sem("ones_made")
        rows_cleared, common_cleared = sem("rows_cleared"), sem("common_cleared")
        a_hi_done, x_hi_done, w_hi_done = sem("a_hi_done"), sem("x_hi_done"), sem("w_hi_done")
        at_copied, low_copied, shared_hi = sem("at_copied"), sem("low_copied"), sem("shared_hi")
        info_ready, common_spread = sem("info_ready"), sem("common_spread")
        acc_hi_done, evacuated = sem("acc_hi_done"), sem("evacuated")
        x_lo_done = [sem("x_lo_done_dve"), sem("x_lo_done_pool")]
        w_lo_done = [sem("w_lo_done_dve"), sem("w_lo_done_pool")]
        dve_step, a_lo_done = sem("dve_step"), sem("a_lo_done")
        in_mask_ready, counts_taken, onehot_ready = sem("in_mask_ready"), sem("counts_taken"), sem("onehot_ready")
        entry_row_taken, entry_a_taken = sem("entry_row_taken"), sem("entry_a_taken")
        fetch_ready, select_ready = sem("fetch_ready"), sem("select_ready")
        a_taken, a_split_ready, low_ready = sem("a_taken"), sem("a_split_ready"), sem("low_ready")
        rows_used, acc_lo_done, shared_ready = sem("rows_used"), sem("acc_lo_done"), sem("shared_ready")
        longest_ready = sem("longest_ready")
        counts_done, at_done, a_done = sem("counts_done"), sem("at_done"), sem("a_done")
        entry_row_done, entry_a_done, low_t_done = sem("entry_row_done"), sem("entry_a_done"), sem("low_t_done")
        x_used, tile_done = sem("x_used"), sem("tile_done")
        over_ready, over_used = sem("over_ready"), sem("over_used")
        over_gathered = [sem(f"over_gathered{i}") for i in range(2)]
        over_stored, over_cleared, over_turn = sem("over_stored"), sem("over_cleared"), sem("over_turn")
        CONSTS = 9

        def x_half(buf, g, half):
            return buf[:, g % 2, half * XH:(half + 1) * XH, 0:samples_of(g)]

        def x_raw_half(g, half):
            n = samples_of(g)
            return x_raw[:, half, 0:XH * n].rearrange("p (k b) -> p k b", b=n)

        def wait_x_lo(eng, g, half):
            eng.wait_ge(x_lo_done[half], g + 1)

        def wait_w_lo(eng, k):
            eng.wait_ge(w_lo_done[k % 2], k // 2 + 1)

        def make_x_lo(eng, g, half):
            eng.wait_ge(x_hi_done, 2 * g + half + 1)
            eng.tensor_tensor(x_half(x_lo, g, half), x_raw_half(g, half), x_half(x_hi, g, half).bitcast(f32),
                              ALU.subtract).then_inc(x_lo_done[half], 1)

        def make_w_lo(eng, k):
            eng.wait_ge(w_hi_done, k + 1)
            eng.tensor_tensor(w_lo[:, k, :], staging[:, k % WSLOTS, :], w_hi[:, k, :].bitcast(f32),
                              ALU.subtract).then_inc(w_lo_done[k % 2], 1)

        block = ctx.enter_context(nc.Block())

        @block.sync
        def _(sp):
            def load_x(g, half):
                if g >= 1:
                    wait_x_lo(sp, g - 1, half)
                n = samples_of(g)
                at = g * KC * GS + half * XH * n
                sp.dma_start(x_raw[:, half, 0:XH * n], x_t[:, at:at + XH * n]).then_inc(x_loaded[half], 16)

            def stage_free(n):
                if n >= WSLOTS:
                    wait_w_lo(sp, n - WSLOTS)

            def load_w(k):
                stage_free(k)
                sp.dma_start(staging[:, k % WSLOTS, :], w_t[:, k, :]).then_inc(w_loaded[k % WSLOTS], 16)

            sp.dma_start(idx_i[:, :], idx).then_inc(idx_loaded, 16)
            sp.dma_start(a_raw[:, :, :], a_t).then_inc(a_loaded, 16)
            load_x(0, 0)
            load_w(0)
            load_x(0, 1)
            for k in range(1, KC):
                load_w(k)
            load_x(1, 0)
            load_x(1, 1)
            stage_free(KC)
            for part in range(3):
                for tab in range(TABLES):
                    at = (part * TABLES + tab) * R
                    sp.dma_start(last_raw[at:at + R, :],
                                 table[(tab + 1) * ROWS - 1, :].rearrange("(r o) -> r o", r=R)).then_inc(last_loaded, 16)
            stage_free(KC + 1)
            for at in (0, R, LO):
                sp.dma_start(common_raw[at:at + R, :], common_t).then_inc(common_loaded, 16)
            for at in (2 * R, LO + R):
                sp.dma_start(common_raw[at:at + 1, :], bias).then_inc(common_loaded, 16)
            for t in range(TILES):
                if t % GT == 0 and t // GT + 2 < GROUPS:
                    load_x(t // GT + 2, 0)
                    load_x(t // GT + 2, 1)
                sp.wait_ge(evacuated, t + 1)
                sp.dma_start(out[t * P:(t + 1) * P, :], out_sb[:, t % 2, :]).then_inc(stored[t % 2], 16)
            for i in range(2):
                sp.wait_ge(stored[i], 16 * (TILES // 2))

        @block.gpsimd
        def _(pool):
            pool.memset(ones, 1.0).then_inc(ones_made, 1)
            pool.memset(in_mask[:, COLS:GROUPS * GC], 0.0).then_inc(consts_ready, 1)
            pool.memset(counts[:, :, :], 0.0).then_inc(consts_ready, 1)
            pool.memset(first[:, :, 0:1], 0.0).then_inc(consts_ready, 1)
            pool.iota(count_f[:, :], pattern=[[1, GS]], base=1, channel_multiplier=0,
                      allow_small_or_imprecise_dtypes=True).then_inc(consts_ready, 1)
            pool.iota(chunk_no[:, :], pattern=[[1, CHUNKS]], base=-CHUNKS, channel_multiplier=0,
                      allow_small_or_imprecise_dtypes=True).then_inc(consts_ready, 1)
            whole = TILES // GT * GT
            pool.iota(sample[:, 0:whole], pattern=[[0, whole // GT], [P, GT]], base=1, channel_multiplier=1,
                      allow_small_or_imprecise_dtypes=True).then_inc(consts_ready, 1)
            pool.iota(sample[:, whole:TILES], pattern=[[P, TILES - whole]], base=1, channel_multiplier=1,
                      allow_small_or_imprecise_dtypes=True).then_inc(consts_ready, 1)
            pool.wait_ge(ones_made, 1)
            pool.affine_select(out=below, in_=ones, compare_op=ALU.is_gt, fill=0.0, base=0,
                               pattern=[[1, P]], channel_multiplier=-1).then_inc(consts_ready, 1)
            pool.affine_select(out=ident[:, :], in_=ones, compare_op=ALU.is_equal, fill=0.0, base=0,
                               pattern=[[1, P]], channel_multiplier=-1).then_inc(consts_ready, 1)
            for s in range(SLOTS):
                pool.memset(rows[:, s, :], 0.0).then_inc(rows_cleared, 1)
            make_x_lo(pool, 0, 1)
            make_w_lo(pool, 1)
            pool.memset(common_w[:, :].bitcast(f32), 0.0).then_inc(common_cleared, 1)
            pool.memset(low[:, :, NL:NL + NC], 0.0).then_inc(common_cleared, 1)
            pool.wait_ge(common_cleared, 2)
            for bias_row in (2 * R, LO + R):
                pool.memset(low[:, :, NL + bias_row:NL + bias_row + 1], 1.0).then_inc(common_cleared, 1)
            pool.wait_ge(rows_cleared, SLOTS)

            def gather(g, chunks):
                pool.wait_ge(fetch_ready, g + 1)
                for c in chunks:
                    n = g * CHUNKS + c
                    if n >= SLOTS:
                        pool.wait_ge(rows_used, n - SLOTS + 1)
                    pool.indirect_dma_start(
                        out=rows[:, n % SLOTS, :], out_offset=None, in_=table_chunks,
                        in_offset=bass.IndirectOffsetOnAxis(ap=fetch[:, g % 2, c:c + 1], axis=0),
                        bounds_check=TABLE_CHUNKS - 1, oob_is_err=False).then_inc(gathered[n % SLOTS], 16)

            gather(0, range(SLOTS))
            make_w_lo(pool, 3)
            make_w_lo(pool, 5)
            gather(0, range(SLOTS, SLOTS + 1))
            make_w_lo(pool, 7)
            gather(0, range(SLOTS + 1, SLOTS + 2))
            make_x_lo(pool, 1, 1)
            gather(0, range(SLOTS + 2, CHUNKS))
            gather(1, range(SLOTS))
            make_x_lo(pool, 2, 1)
            gather(1, range(SLOTS, CHUNKS))
            for g in range(2, GROUPS):
                gather(g, range(CHUNKS))
                if g + 1 < GROUPS:
                    make_x_lo(pool, g + 1, 1)

            pool.wait_ge(longest_ready, 1)
            for i in range(2):
                pool.wait_ge(stored[i], 16 * (TILES // 2))
            last_chunk = pool.to_reg(TABLE_CHUNKS - 1)
            with pool.If(pool.value_load(longest_i[0:1, 0:1], min_val=0, max_val=GC * P) > P):
                pool.sem_inc(over_turn, 1)
                with pool.Fori(0, TILES) as t:
                    pool.wait_ge(over_ready, t + 1)
                    pool.sem_inc(over_cleared, 1)
                    for n in range(TABLES * CHUNKS):
                        if n >= 2:
                            pool.wait_ge(over_used, t * (TABLES * CHUNKS) + n - 1)
                            pool.sem_inc(over_cleared, 1)
                        pool.indirect_dma_start(
                            out=rows[:, n % 2, :], out_offset=None, in_=table_chunks,
                            in_offset=bass.IndirectOffsetOnAxis(
                                ap=over_fetch[:, n // CHUNKS, n % CHUNKS:n % CHUNKS + 1], axis=0),
                            bounds_check=last_chunk, oob_is_err=False).then_inc(over_gathered[n % 2], 16)
                    pool.wait_ge(over_used, (t + 1) * (TABLES * CHUNKS))
                    pool.sem_inc(over_cleared, 1)
                    pool.dma_start(out[bass.ds(t * P, P), :], acc, accum_op=ALU.add).then_inc(over_stored, 16)
                    pool.wait_ge(over_stored, t * 16 + 16)
                    pool.sem_inc(over_turn, 1)

        @block.scalar
        def _(act):
            def make_x_hi(g, half):
                act.wait_ge(x_loaded[half], 16 * (g + 1))
                if g >= 2:
                    act.wait_ge(x_used, g - 1)
                act.activation(x_half(x_hi, g, half), x_raw_half(g, half), ACT.Copy).then_inc(x_hi_done, 1)

            def make_w_hi(k):
                act.wait_ge(w_loaded[k % WSLOTS], 16 * (k // WSLOTS + 1))
                act.activation(w_hi[:, k, :], staging[:, k % WSLOTS, :], ACT.Copy).then_inc(w_hi_done, 1)

            def copy_at(g):
                act.wait_ge(at_done, g + 1)
                if g >= 1:
                    act.wait_ge(a_done, g)
                n = samples_of(g)
                act.activation(at_sb[:, 0:n], at_ps[:, 0:n], ACT.Copy).then_inc(at_copied, 1)

            def spread_a(g):
                act.wait_ge(a_split_ready, 2 * (g + 1))
                ts, n = tiles_of(g), len(tiles_of(g))
                split = a_split[:, 0:n, :, :].rearrange("p t s r -> p t (s r)")
                act.activation(info[:, ts[0]:ts[-1] + 1, :, 2:INFO],
                               split.unsqueeze(2).broadcast_to([P, n, TABLES, 2 * R]), ACT.Copy).then_inc(info_ready, 1)
                if g == 0:
                    act.wait_ge(common_cleared, 4)
                else:
                    act.wait_ge(low_t_done, g)
                act.activation(low[:, 0:n, NL:NL + 2 * R], split, ACT.Copy).then_inc(common_spread, 1)
                act.activation(low[:, 0:n, NL + LO:NL + LO + R], a_split[:, 0:n, 0, :], ACT.Copy).then_inc(common_spread, 1)

            def copy_low(g):
                act.wait_ge(low_t_done, g + 1)
                if g >= 2:
                    act.wait_ge(tile_done, GT * (g - 1))
                n = samples_of(g)
                act.activation(last_t[:, g % 2, 0:n], last_ps[:, 0:n], ACT.Copy).then_inc(low_copied, 1)
                act.activation(common_a[:, g % 2, 0:n], common_ps[:, 0:n], ACT.Copy).then_inc(low_copied, 1)

            def make_acc_hi(g):
                act.wait_ge(rows_used, CHUNKS * (g + 1))
                if g >= 1:
                    act.wait_ge(tile_done, GT * g)
                act.activation(acc_hi[:, :], acc, ACT.Copy).then_inc(acc_hi_done, 1)

            def evacuate(t):
                act.wait_ge(tile_done, t + 1)
                if t >= 2:
                    act.wait_ge(stored[t % 2], 16 * (t // 2))
                act.activation(out_sb[:, t % 2, :], main_ps[t % GT][:, :], ACT.Copy).then_inc(evacuated, 1)

            act.wait_ge(a_loaded, 16)
            act.activation(a_hl[:, :, 0:R], a_raw[:, :, :], ACT.Copy, scale=2.0).then_inc(a_hi_done, 1)
            make_x_hi(0, 0)
            make_w_hi(0)
            make_x_hi(0, 1)
            make_w_hi(1)
            make_w_hi(2)
            copy_at(0)
            make_w_hi(3)
            spread_a(0)
            make_w_hi(4)
            copy_low(0)
            make_w_hi(5)
            make_w_hi(6)
            make_w_hi(7)
            make_x_hi(1, 0)
            make_x_hi(1, 1)
            act.wait_ge(last_loaded, 16 * 3 * TABLES)
            act.activation(last_w[:, :], last_raw, ACT.Copy).then_inc(shared_hi, 1)
            act.wait_ge(common_loaded, 16 * 5)
            act.activation(common_w[0:CH, :], common_raw[0:CH, :], ACT.Copy).then_inc(shared_hi, 1)
            act.activation(common_w[LO:NC, :], common_raw[LO:NC, :], ACT.Copy).then_inc(shared_hi, 1)
            copy_at(1)
            make_acc_hi(0)
            evacuate(0)
            spread_a(1)
            make_x_hi(2, 0)
            make_x_hi(2, 1)
            evacuate(1)
            evacuate(2)
            copy_low(1)
            copy_at(2)
            make_acc_hi(1)
            evacuate(3)
            evacuate(4)
            spread_a(2)
            copy_low(2)
            for g in range(2, GROUPS):
                t, more = g * GT, g + 1 < GROUPS
                if more:
                    make_x_hi(g + 1, 0)
                    make_x_hi(g + 1, 1)
                    copy_at(g + 1)
                evacuate(t - 1)
                make_acc_hi(g)
                if more:
                    spread_a(g + 1)
                evacuate(t)
                if more:
                    copy_low(g + 1)
                    evacuate(t + 1)

        @block.vector
        def _(dve):
            steps = [0]

            def link(ins):
                steps[0] += 1
                ins.then_inc(dve_step, 1)
                dve.wait_ge(dve_step, steps[0])

            def take_a(g):
                ts, n = tiles_of(g), len(tiles_of(g))
                t0, t1 = ts[0], ts[-1] + 1
                dve.wait_ge(a_done, g + 1)
                link(dve.tensor_copy(a_part[:, 0:n, :], a_ps[:, 0:n, 0:R]))
                dve.tensor_tensor(a_all[:, t0:t1, :], a_part[:, 0:n, :], a_ps[:, 0:n, R:2 * R],
                                  ALU.add).then_inc(a_taken, 1)
                dve.wait_ge(a_taken, g + 1)
                if g >= 1:
                    dve.wait_ge(common_spread, 2 * g)
                dve.tensor_copy(a_split[:, 0:n, 0, :].bitcast(f32r), a_all[:, t0:t1, :]).then_inc(a_split_ready, 1)
                dve.wait_ge(a_split_ready, 2 * g + 1)
                dve.tensor_tensor(a_split[:, 0:n, 1, :].bitcast(f32r), a_all[:, t0:t1, :], a_split[:, 0:n, 0, :],
                                  ALU.subtract).then_inc(a_split_ready, 1)
                dve.wait_ge(a_split_ready, 2 * (g + 1))
                if g >= 1:
                    dve.wait_ge(low_t_done, g)
                both = [P, n, TABLES, R]
                mask = last_mask[:, t0 * TABLES:t1 * TABLES].rearrange("p (t u) -> p t u", u=TABLES)
                mask = mask.unsqueeze(3).broadcast_to(both)
                for part, which in enumerate((0, 1, 0)):
                    masked = low[:, 0:n, part * TABLES * R:(part + 1) * TABLES * R]
                    dve.tensor_tensor(masked.rearrange("p t (u r) -> p t u r", u=TABLES),
                                      a_split[:, 0:n, which, :].unsqueeze(2).broadcast_to(both), mask,
                                      ALU.mult).then_inc(low_ready, 1)

            def make_onehot(g):
                if g >= 1:
                    dve.wait_ge(entry_a_done, g)
                n = len(tiles_of(g)) * TABLES
                dve.tensor_tensor(onehot[:, 0:n, :], count_f[:, 0:P].unsqueeze(1).broadcast_to([P, n, P]),
                                  place[:, g * GC:g * GC + n].unsqueeze(2).broadcast_to([P, n, P]),
                                  ALU.is_equal).then_inc(onehot_ready, 1)

            def take_rows(g):
                dve.wait_ge(entry_row_done, g + 1)
                dve.tensor_copy(entry_row[:, :], entry_row_ps).then_inc(entry_row_taken, 1)
                dve.wait_ge(entry_row_taken, g + 1)
                link(dve.tensor_copy(entry_sample[:, g:g + 1], entry_row[:, 0:1]))
                link(dve.tensor_scalar(first_chunk[:, :], entry_row[:, 1:2], 0.0, ABSENT, ALU.is_equal, ALU.mult))
                link(dve.tensor_scalar(first_chunk[:, :], first_chunk[:, :], entry_row[:, 1:2], float(CHUNKS),
                                       ALU.add, ALU.mult))
                dve.tensor_scalar(fetch[:, g % 2, :], chunk_no[:, :], first_chunk[:, 0:1], None,
                                  ALU.add).then_inc(fetch_ready, 1)

            def take_entries(g):
                dve.wait_ge(entry_a_done, g + 1)
                dve.tensor_copy(entry_a[:, :], entry_a_ps).then_inc(entry_a_taken, 1)
                dve.wait_ge(entry_a_taken, g + 1)
                link(dve.tensor_tensor(a_entry[:, :], entry_a[:, 0:R], entry_a[:, R:2 * R], ALU.add))
                if g >= 2:
                    dve.wait_ge(tile_done, GT * (g - 1))
                n = samples_of(g)
                dve.tensor_scalar(select[:, g % 2, 0:n], count_f[:, 0:n], entry_sample[:, g:g + 1], None,
                                  ALU.is_equal).then_inc(select_ready, 1)

            def multiply_rows(rows_r, a_r, start):
                if start:
                    return dve.tensor_scalar(acc, rows_r, a_r, None, ALU.mult)
                return dve.scalar_tensor_tensor(acc, rows_r, a_r, acc, ALU.mult, ALU.add)

            def row_products(g, chunks):
                for c in chunks:
                    n = g * CHUNKS + c
                    dve.wait_ge(gathered[n % SLOTS], 16 * (n // SLOTS + 1))
                    for j in range(RB):
                        r = c * RB + j
                        ins = multiply_rows(rows[:, n % SLOTS, j * OUT_F:(j + 1) * OUT_F], a_entry[:, r:r + 1], r == 0)
                        if j < RB - 1:
                            link(ins)
                    ins.then_inc(rows_used, 1)
                    dve.wait_ge(rows_used, n + 1)

            def make_acc_lo(g):
                if g >= 1:
                    dve.wait_ge(tile_done, GT * g)
                dve.wait_ge(acc_hi_done, g + 1)
                dve.tensor_tensor(acc_lo[:, :], acc, acc_hi[:, :].bitcast(f32), ALU.subtract).then_inc(acc_lo_done, 1)
                dve.wait_ge(acc_lo_done, g + 1)

            dve.wait_ge(a_hi_done, 1)
            dve.scalar_tensor_tensor(a_hl[:, :, R:2 * R], a_raw[:, :, :], 2.0, a_hl[:, :, 0:R].bitcast(f32),
                                     ALU.mult, ALU.subtract).then_inc(a_lo_done, 1)
            dve.wait_ge(idx_loaded, 16)
            link(dve.tensor_copy(row[:, :], idx_i[:, :]))
            link(dve.tensor_scalar(wrap[:, :], row[:, :], 0.0, float(ROWS), ALU.is_lt, ALU.mult))
            link(dve.tensor_tensor(row[:, :], row[:, :], wrap[:, :], ALU.add))
            link(dve.tensor_scalar(row[:, :], row[:, :], 0.0, float(ROWS - 1), ALU.max, ALU.min))
            dve.wait_ge(consts_ready, CONSTS)
            dve.tensor_scalar(in_mask[:, 0:COLS], row[:, :], float(ROWS - 1), None, ALU.is_lt).then_inc(in_mask_ready, 1)
            make_x_lo(dve, 0, 0)
            make_w_lo(dve, 0)
            link(dve.tensor_scalar(last_mask[:, :], row[:, :], float(ROWS - 1), None, ALU.is_ge))
            row_v = row[:, :].rearrange("p (t u) -> p t u", u=TABLES)
            for tab in range(TABLES):
                link(dve.tensor_scalar(row_v[:, :, tab], row_v[:, :, tab], float(tab * ROWS + 1), None, ALU.add))
            link(dve.tensor_copy(info[:, :, :, 1], row_v))
            link(dve.tensor_copy(info[:, :, :, 0], sample[:, :].unsqueeze(2).broadcast_to([P, TILES, TABLES])))
            dve.wait_ge(counts_done, 1)
            dve.tensor_copy(counts[:, :, 0:COLS], counts_ps.rearrange("p (s c) -> p s c", s=2)).then_inc(counts_taken, 1)
            dve.wait_ge(counts_taken, 1)
            total = counts[:, 1, :].rearrange("p (g j) -> p g j", j=GC)
            for j in range(GC):
                link(dve.tensor_tensor(first[:, :, j + 1], first[:, :, j], total[:, :, j], ALU.add))
            place_v = place[:, :].rearrange("p (g j) -> p g j", j=GC)
            link(dve.tensor_tensor(place_v, counts[:, 0, :].rearrange("p (g j) -> p g j", j=GC),
                                   first[:, :, 0:GC], ALU.add))
            dve.wait_ge(in_mask_ready, 1)
            link(dve.scalar_tensor_tensor(place[:, :], place[:, :], 1.0, in_mask[:, :], ALU.add, ALU.mult))
            make_onehot(0)
            make_w_lo(dve, 2)
            take_rows(0)
            take_a(0)
            make_w_lo(dve, 4)
            take_entries(0)
            make_onehot(1)
            row_products(0, range(0, 2))
            make_w_lo(dve, 6)
            row_products(0, range(2, 4))
            take_rows(1)
            make_x_lo(dve, 1, 0)
            row_products(0, range(4, CHUNKS))
            dve.wait_ge(shared_hi, 3)
            dve.tensor_tensor(last_w[LO:NL, :], last_raw[LO:NL, :], last_w[LO:NL, :].bitcast(f32),
                              ALU.subtract).then_inc(shared_ready, 1)
            dve.tensor_tensor(common_w[LO:NC, :], common_raw[LO:NC, :], common_w[LO:NC, :].bitcast(f32),
                              ALU.subtract).then_inc(shared_ready, 1)
            make_acc_lo(0)
            take_a(1)
            take_entries(1)
            make_onehot(2)
            row_products(1, range(0, 4))
            make_x_lo(dve, 2, 0)
            take_rows(2)
            row_products(1, range(4, CHUNKS))
            make_acc_lo(1)
            take_a(2)
            take_entries(2)
            for g in range(2, GROUPS):
                more = g + 1 < GROUPS
                if more:
                    make_onehot(g + 1)
                row_products(g, range(0, 4))
                if more:
                    take_rows(g + 1)
                row_products(g, range(4, CHUNKS - 1))
                if more:
                    make_x_lo(dve, g + 1, 0)
                row_products(g, range(CHUNKS - 1, CHUNKS))
                if more:
                    take_a(g + 1)
                make_acc_lo(g)
                if more:
                    take_entries(g + 1)

            link(dve.tensor_reduce(longest[:, :], first[:, :, GC], axis=AX.X, op=ALU.max))
            dve.tensor_copy(longest_i[:, :], longest[:, :]).then_inc(longest_ready, 1)
            dve.wait_ge(longest_ready, 1)
            with dve.If(dve.value_load(longest_i[0:1, 0:1], min_val=0, max_val=GC * P) > P):
                link(dve.tensor_scalar(over[:, :], place[:, 0:COLS], float(P), None, ALU.is_gt))
                link(dve.tensor_scalar(over_chunk[:, :], over[:, :], -ABSENT, ABSENT, ALU.mult, ALU.add))
                link(dve.tensor_tensor(over_chunk[:, :], over_chunk[:, :], row[:, :], ALU.add))
                link(dve.tensor_scalar(over_chunk[:, :], over_chunk[:, :], float(CHUNKS), None, ALU.mult))
                link(dve.tensor_tensor(over_fetch_all[:, :, :],
                                       over_chunk[:, :].unsqueeze(2).broadcast_to([P, COLS, CHUNKS]),
                                       chunk_no[:, :].unsqueeze(1).broadcast_to([P, COLS, CHUNKS]), ALU.add))
                with dve.Fori(0, TILES) as t:
                    before = steps[0]
                    per_turn = TABLES + TABLES * (R - CHUNKS)

                    def turn_link(ins, n):
                        ins.then_inc(dve_step, 1)
                        dve.wait_ge(dve_step, t * per_turn + (before + n))

                    dve.wait_ge(over_turn, t + 1)
                    for tab in range(TABLES):
                        turn_link(dve.tensor_scalar(over_a[:, tab, :], a_all[:, bass.ds(t, 1), :].squeeze(1),
                                                    over[:, bass.ds(t * TABLES + tab, 1)], None, ALU.mult), tab + 1)
                    dve.tensor_copy(over_fetch[:, :, :],
                                    over_fetch_all[:, bass.ds(t * TABLES, TABLES), :]).then_inc(over_ready, 1)
                    links = TABLES
                    for n in range(TABLES * CHUNKS):
                        tab, c = divmod(n, CHUNKS)
                        dve.wait_ge(over_gathered[n % 2], t * (16 * TABLES * CHUNKS // 2) + 16 * (n // 2 + 1))
                        for j in range(RB):
                            r = c * RB + j
                            ins = multiply_rows(rows[:, n % 2, j * OUT_F:(j + 1) * OUT_F], over_a[:, tab, r:r + 1],
                                                n == 0 and j == 0)
                            if j < RB - 1:
                                links += 1
                                turn_link(ins, links)
                        ins.then_inc(over_used, 1)
                        dve.wait_ge(over_used, t * (TABLES * CHUNKS) + n + 1)

        @block.tensor
        def _(pe):
            def rank_a(g):
                wait_x_lo(pe, g, 0)
                wait_x_lo(pe, g, 1)
                pe.wait_ge(entry_row_taken, g + 1)
                if g >= 1:
                    pe.wait_ge(low_copied, 2 * g)
                n = samples_of(g)
                for k in range(KC):
                    pe.matmul(at_ps[:, 0:n], a_hl[:, k, :], x_hi[:, g % 2, k, 0:n], start=(k == 0), stop=False)
                    last = pe.matmul(at_ps[0:R, 0:n], a_hl[:, k, 0:R], x_lo[:, g % 2, k, 0:n], start=False,
                                     stop=(k == KC - 1))
                last.then_inc(at_done, 1)

            def transpose_a(g):
                pe.wait_ge(at_copied, g + 1)
                if g == 0:
                    pe.wait_ge(counts_taken, 1)
                else:
                    pe.wait_ge(low_copied, 2 * g)
                for j in range(len(tiles_of(g))):
                    last = pe.transpose(a_ps[:, j, :], at_sb[:, j * P:(j + 1) * P], ident[0:2 * R, 0:2 * R])
                last.then_inc(a_done, 1)

            def pack_rows(g):
                pe.wait_ge(onehot_ready, g + 1)
                if g >= 1:
                    pe.wait_ge(low_copied, 2 * g)
                cols = [(t, tab) for t in tiles_of(g) for tab in range(TABLES)]
                for c, (t, tab) in enumerate(cols):
                    last = pe.matmul(entry_row_ps, onehot[:, c, :], info[:, t, tab, 0:2], start=(c == 0),
                                     stop=(c == len(cols) - 1))
                last.then_inc(entry_row_done, 1)

            def pack_a(g):
                pe.wait_ge(info_ready, g + 1)
                pe.wait_ge(at_copied, g + 1)
                cols = [(t, tab) for t in tiles_of(g) for tab in range(TABLES)]
                for c, (t, tab) in enumerate(cols):
                    last = pe.matmul(entry_a_ps, onehot[:, c, :], info[:, t, tab, 2:INFO], start=(c == 0),
                                     stop=(c == len(cols) - 1))
                last.then_inc(entry_a_done, 1)

            def transpose_low(g):
                pe.wait_ge(low_ready, 3 * (g + 1))
                pe.wait_ge(common_spread, 2 * (g + 1))
                pe.wait_ge(entry_a_taken, g + 1)
                for j in range(len(tiles_of(g))):
                    to = slice(j * P, (j + 1) * P)
                    pe.transpose(last_ps[:, to], low[:, j, 0:NL], ident[:, :])
                    last = pe.transpose(common_ps[:, to], low[:, j, NL:NL + NC], ident[:, :])
                last.then_inc(low_t_done, 1)

            def base_step(t, half, k):
                g, j = divmod(t, GT)
                to = main_ps[t % GT][:, half * BANK:(half + 1) * BANK]
                b, o = slice(j * P, (j + 1) * P), slice(half * BANK, (half + 1) * BANK)
                pe.matmul(to, x_hi[:, g % 2, k, b], w_hi[:, k, o], start=(k == 0), stop=False)
                pe.matmul(to, x_hi[:, g % 2, k, b], w_lo[:, k, o], start=False, stop=False)
                return pe.matmul(to, x_lo[:, g % 2, k, b], w_hi[:, k, o], start=False, stop=False)

            def base(t, half):
                g = t // GT
                wait_x_lo(pe, g, 0)
                wait_x_lo(pe, g, 1)
                pe.wait_ge(evacuated, t - GT + 1)
                for k in range(KC):
                    last = base_step(t, half, k)
                if half == HALVES - 1 and t == tiles_of(g)[-1]:
                    last.then_inc(x_used, 1)

            def finish(t):
                g, j = divmod(t, GT)
                b = slice(j * P, (j + 1) * P)
                pe.wait_ge(shared_ready, 2)
                pe.wait_ge(low_copied, 2 * (g + 1))
                for half in range(HALVES):
                    o = slice(half * BANK, (half + 1) * BANK)
                    pe.matmul(main_ps[t % GT][:, o], last_t[:, g % 2, b], last_w[:, o], start=False, stop=False)
                    pe.matmul(main_ps[t % GT][:, o], common_a[:, g % 2, b], common_w[:, o], start=False, stop=False)
                pe.wait_ge(select_ready, g + 1)
                pe.wait_ge(acc_lo_done, g + 1)
                for half in range(HALVES):
                    o = slice(half * BANK, (half + 1) * BANK)
                    pe.matmul(main_ps[t % GT][:, o], select[:, g % 2, b], acc_hi[:, o], start=False, stop=False)
                    last = pe.matmul(main_ps[t % GT][:, o], select[:, g % 2, b], acc_lo[:, o], start=False, stop=True)
                last.then_inc(tile_done, 1)

            pe.wait_ge(consts_ready, CONSTS)
            pe.wait_ge(ones_made, 1)
            pe.wait_ge(in_mask_ready, 1)
            pe.matmul(counts_ps[:, 0:COLS], below, in_mask[:, 0:COLS], start=True, stop=True)
            pe.matmul(counts_ps[:, COLS:2 * COLS], ones, in_mask[:, 0:COLS], start=True,
                      stop=True).then_inc(counts_done, 1)
            def first_group(k, tiles):
                wait_x_lo(pe, 0, k // XH)
                wait_w_lo(pe, k)
                for t in tiles:
                    for half in range(HALVES):
                        last = base_step(t, half, k)
                return last

            first_group(0, range(0, 3))
            pack_rows(0)
            pe.wait_ge(a_lo_done, 1)
            rank_a(0)
            first_group(1, range(0, 1))
            transpose_a(0)
            first_group(1, range(1, 3))
            pack_a(0)
            first_group(2, range(0, 3))
            transpose_low(0)
            first_group(3, range(0, 3))
            first_group(4, range(0, 3))
            pack_rows(1)
            first_group(5, range(0, 3))
            first_group(6, range(0, 3))
            rank_a(1)
            first_group(7, range(0, 3)).then_inc(x_used, 1)
            finish(0)
            transpose_a(1)
            base(3, 0)
            finish(1)
            pack_a(1)
            base(3, 1)
            finish(2)
            transpose_low(1)
            base(4, 0)
            pack_rows(2)
            base(4, 1)
            rank_a(2)
            base(5, 0)
            transpose_a(2)
            base(5, 1)
            finish(3)
            finish(4)
            pack_a(2)
            transpose_low(2)
            pack_rows(3)
            for g in range(2, GROUPS):
                t, more = g * GT, g + 1 < GROUPS
                base(t, 0)
                base(t, 1)
                if more:
                    rank_a(g + 1)
                finish(t - 1)
                if more:
                    transpose_a(g + 1)
                    base(t + 1, 0)
                    pack_a(g + 1)
                    base(t + 1, 1)
                finish(t)
                if more:
                    transpose_low(g + 1)
                    base(t + 2, 0)
                    if g + 2 < GROUPS:
                        pack_rows(g + 2)
                    base(t + 2, 1)
                    finish(t + 1)


def kernel(**inputs):
    import numpy as np
    import concourse.bacc as bacc
    from concourse.bass_utils import run_bass_kernel_spmd

    a = {k: np.asarray(v) for k, v in inputs.items()}
    idx = np.stack([a["r_user_indices"].reshape(TILES, P), a["r_item_indices"].reshape(TILES, P)], axis=-1)
    x = a["r_x"].reshape(BATCH, KC, P).transpose(2, 1, 0)
    x_t = np.concatenate([x[:, :, g * GS:g * GS + samples_of(g)].reshape(P, -1) for g in range(GROUPS)], axis=1)
    tables = np.concatenate([a["L0_rec_B_user"], a["L0_rec_B_item"]], axis=0).transpose(0, 2, 1)
    arrays = {
        "idx": idx.transpose(1, 0, 2).reshape(P, COLS),
        "x_t": x_t,
        "w_t": a["L0_rec_W_base"].reshape(OUT_F, KC, P).transpose(2, 1, 0),
        "a_t": a["L0_rec_A"].reshape(R, KC, P).transpose(2, 1, 0),
        "bias": a["L0_rec_b_base"].reshape(1, OUT_F),
        "common_t": a["L0_rec_W_common"].T,
        "table": tables.reshape(TABLES * ROWS, R * OUT_F),
    }
    arrays = {k: np.ascontiguousarray(v) for k, v in arrays.items()}
    nc = bacc.Bacc("TRN2", target_bir_lowering=False, num_devices=1)
    args = [nc.dram_tensor(k, v.shape, mybir.dt.from_np(v.dtype), kind="ExternalInput").ap() for k, v in arrays.items()]
    args.append(nc.dram_tensor("out", (BATCH, OUT_F), mybir.dt.float32, kind="ExternalOutput").ap())
    rec_kernel(nc, *args)
    return run_bass_kernel_spmd(nc, [arrays], core_ids=[0]).results[0]["out"]
```

```python
from contextlib import ExitStack

import concourse.bass as bass
from concourse import mybir

P = 128
BATCH, IN_F, OUT_F, R = 2048, 1024, 1024, 16
ROWS = 1250
TABLES = 2
KC = IN_F // P
BANK = 512
HALVES = OUT_F // BANK
TILES = BATCH // P
GT = 3
GROUPS = -(-TILES // GT)
SHORT = TILES - (GROUPS - 1) * GT
GS = GT * P
COLS = TILES * TABLES
GC = GT * TABLES
PAD = GROUPS * GC - COLS
COPIES = 2
PLACES = P // COPIES
RB = 2
CHUNKS = R // RB
CHUNK = RB * OUT_F
SLOTS = 3
WSLOTS = 3
X0, W0, LAST, COMMON = 0, 1, 1 + KC, 2 + KC
LO_BY_POOL = (W0, W0 + 3, W0 + 5, W0 + 6, W0 + 7)
XH = KC // 2
ABSENT = float(1 << 16)
TABLE_CHUNKS = TABLES * ROWS * CHUNKS
INFO = 2 + 2 * R
LO = 64
NL = LO + TABLES * R
NC = LO + R + 1
CH = 2 * R + 1


def tiles_of(g):
    return range(max(0, SHORT + (g - 1) * GT), SHORT + g * GT)


def samples_of(g):
    return len(tiles_of(g)) * P


def place_of(t):
    g = (t + GT - SHORT) // GT
    return g, t - tiles_of(g)[0]


def chunks_of(g):
    return CHUNKS // COPIES if g == 0 else CHUNKS


def chunks_before(g):
    return sum(chunks_of(h) for h in range(g))


def rec_kernel(nc, idx, x_t, w_t, a_t, bias, common_t, table, out):
    f32, f32r, i32 = mybir.dt.float32, mybir.dt.float32r, mybir.dt.int32
    ALU, ACT, AX = mybir.AluOpType, mybir.ActivationFunctionType, mybir.AxisListType
    table_chunks = table.rearrange("n (c k) -> (n c) k", c=CHUNKS)

    ctx = ExitStack()
    with ctx:
        def sb(name, shape, dt=f32):
            return ctx.enter_context(nc.sbuf_tensor(name, shape, dt))

        def pb(name, shape):
            return ctx.enter_context(nc.psum_tensor(name, shape, f32))

        def sem(name):
            return ctx.enter_context(nc.semaphore(name))

        w_hi = sb("w_hi", [P, KC, OUT_F], f32r)
        w_lo = sb("w_lo", [P, KC, OUT_F], f32r)
        x_raw = sb("x_raw", [P, 2, XH * GS])
        x_hi = sb("x_hi", [P, 2, KC, GS], f32r)
        x_lo = sb("x_lo", [P, 2, KC, GS], f32r)
        a_raw = sb("a_raw", [P, KC, R])
        a_hl = sb("a_hl", [P, KC, 2 * R], f32r)
        last_w = sb("last_w", [NL, OUT_F], f32r)
        common_w = sb("common_w", [NC, OUT_F], f32r)
        at_sb = sb("at_sb", [2 * R, GS])
        a_part = sb("a_part", [P, GT, R])
        a_all = sb("a_all", [P, TILES, R])
        a_split = sb("a_split", [P, GT, 2, R])
        low = sb("low", [P, GT, NL + NC])
        last_t = sb("last_t", [NL, 2, GS], f32r)
        common_a = sb("common_a", [NC, 2, GS], f32r)
        idx_i = sb("idx_i", [P, COLS], i32)
        row = sb("row", [P, COLS])
        wrap = sb("wrap", [P, COLS])
        in_mask = sb("in_mask", [P, GROUPS * GC])
        last_mask = sb("last_mask", [P, COLS])
        counts = sb("counts", [P, 2, GROUPS * GC])
        first = sb("first", [P, GROUPS, GC + 1])
        place = sb("place", [P, GROUPS * GC])
        info = sb("info", [P, TILES, TABLES, INFO], f32r)
        sample = sb("sample", [P, TILES])
        count_f = sb("count_f", [P, GS])
        ident = sb("ident", [P, P])
        onehot = sb("onehot", [P, GC, P], f32r)
        entry_row = sb("entry_row", [P, 2])
        entry_sample = sb("entry_sample", [P, GROUPS])
        entry_a = sb("entry_a", [P, 2 * R])
        a_entry = sb("a_entry", [P, R])
        first_chunk = sb("first_chunk", [P, 1])
        chunk_no = sb("chunk_no", [P, CHUNKS])
        half_no = sb("half_no", [P, CHUNKS // COPIES])
        fetch = sb("fetch", [P, 2, CHUNKS], i32)
        select = sb("select", [P, 2, GS], f32r)
        onehot_0 = select[:, 1, 0:SHORT * TABLES * P].rearrange("p (c k) -> p c k", k=P)
        rows = sb("rows", [P, SLOTS, CHUNK])
        staging = sb("staging", [P, WSLOTS, OUT_F])
        out_sb = staging[:, 0:2, :]
        acc_sb = sb("acc", [P, OUT_F])
        acc = acc_sb[:, :]
        ones, below, count_0 = (acc_sb[:, i * P:(i + 1) * P] for i in range(3))
        x0_raw = staging[:, X0 % WSLOTS, 0:KC * SHORT * P].rearrange("p (k b) -> p k b", k=KC)
        last_raw = staging[0:NL, LAST % WSLOTS, :]
        common_raw = staging[0:NC, COMMON % WSLOTS, :]
        acc_hi = sb("acc_hi", [P, OUT_F], f32r)
        acc_lo = sb("acc_lo", [P, OUT_F], f32r)
        longest = sb("longest", [P, 1])
        longest_i = sb("longest_i", [P, 1], i32)
        over = sb("over", [P, COLS])
        over_chunk = sb("over_chunk", [P, COLS])
        over_fetch_all = x_raw[:, 0, 0:COLS * CHUNKS].bitcast(i32).rearrange("p (c k) -> p c k", k=CHUNKS)
        over_fetch = sb("over_fetch", [P, TABLES, CHUNKS], i32)
        over_a = sb("over_a", [P, TABLES, R])

        main_ps = [pb(f"main_ps{i}", [P, OUT_F]) for i in range(GT)]
        ps_a = pb("ps_a", [P, BANK])
        ps_b = pb("ps_b", [P, BANK])
        at_ps = ps_a[0:2 * R, 0:GS]
        common_ps = ps_a[0:NC, 0:GS]
        entry_row_ps = ps_a[:, GS:GS + 2]
        entry_a_ps = ps_a[:, GS:GS + 2 * R]
        a_ps = ps_b[:, 0:GT * 2 * R].rearrange("p (t r) -> p t r", r=2 * R)
        counts_ps = ps_b[:, 0:2 * COLS]
        last_ps = ps_b[0:NL, P:P + GS]

        idx_loaded, a_loaded = sem("idx_loaded"), sem("a_loaded")
        last_loaded, common_loaded = sem("last_loaded"), sem("common_loaded")
        x_loaded = [sem(f"x_loaded{i}") for i in range(2)]
        staged = [sem(f"staged{i}") for i in range(WSLOTS)]
        gathered = [sem(f"gathered{i}") for i in range(SLOTS)]
        stored = [sem(f"stored{i}") for i in range(2)]
        consts_ready, ones_made = sem("consts_ready"), sem("ones_made")
        rows_cleared, common_cleared = [sem("rows_cleared_dve"), sem("rows_cleared_pool")], sem("common_cleared")
        a_hi_done, x_hi_done, staged_hi = sem("a_hi_done"), sem("x_hi_done"), sem("staged_hi")
        at_copied, low_copied, shared_hi = sem("at_copied"), sem("low_copied"), sem("shared_hi")
        info_ready, common_spread = sem("info_ready"), sem("common_spread")
        acc_hi_done, evacuated = sem("acc_hi_done"), sem("evacuated")
        x_lo_done = [sem("x_lo_done_dve"), sem("x_lo_done_pool")]
        staged_lo = [sem("staged_lo_dve"), sem("staged_lo_pool")]
        dve_step, a_lo_done = sem("dve_step"), sem("a_lo_done")
        in_mask_ready, counts_taken, onehot_ready = sem("in_mask_ready"), sem("counts_taken"), sem("onehot_ready")
        entry_row_taken, entry_a_taken = sem("entry_row_taken"), sem("entry_a_taken")
        fetch_ready, select_ready = sem("fetch_ready"), sem("select_ready")
        a_taken, a_split_ready, low_ready = sem("a_taken"), sem("a_split_ready"), sem("low_ready")
        rows_used, acc_lo_done, shared_ready = sem("rows_used"), sem("acc_lo_done"), sem("shared_ready")
        longest_ready = sem("longest_ready")
        counts_done, at_done, a_done = sem("counts_done"), sem("at_done"), sem("a_done")
        entry_row_done, entry_a_done, low_t_done = sem("entry_row_done"), sem("entry_a_done"), sem("low_t_done")
        x_used, tile_done = sem("x_used"), sem("tile_done")
        over_ready, over_used = sem("over_ready"), sem("over_used")
        over_gathered = [sem(f"over_gathered{i}") for i in range(2)]
        over_stored, over_cleared, over_turn = sem("over_stored"), sem("over_cleared"), sem("over_turn")
        CONSTS = 13

        def x_half(buf, g, half):
            return buf[:, g % 2, half * XH:(half + 1) * XH, 0:samples_of(g)]

        def x_raw_half(g, half):
            n = samples_of(g)
            return x_raw[:, half, 0:XH * n].rearrange("p (k b) -> p k b", b=n)

        def wait_staged_lo(eng, n):
            who = int(n in LO_BY_POOL)
            eng.wait_ge(staged_lo[who], sum(int(m in LO_BY_POOL) == who for m in range(n + 1)))

        def make_staged_lo(eng, n):
            eng.wait_ge(staged_hi, n + 1)
            hi, lo, raw = ((x_hi[:, 0, :, 0:SHORT * P], x_lo[:, 0, :, 0:SHORT * P], x0_raw) if n == X0 else
                           (w_hi[:, n - W0, :], w_lo[:, n - W0, :], staging[:, n % WSLOTS, :]))
            eng.tensor_tensor(lo, raw, hi.bitcast(f32), ALU.subtract).then_inc(staged_lo[int(n in LO_BY_POOL)], 1)

        def wait_x_lo(eng, g, half):
            if g == 0:
                wait_staged_lo(eng, X0)
            else:
                eng.wait_ge(x_lo_done[half], g)

        def make_x_lo(eng, g, half):
            eng.wait_ge(x_hi_done, 2 * (g - 1) + half + 1)
            eng.tensor_tensor(x_half(x_lo, g, half), x_raw_half(g, half), x_half(x_hi, g, half).bitcast(f32),
                              ALU.subtract).then_inc(x_lo_done[half], 1)

        def stores(i):
            return 16 * (TILES // 2 + (HALVES - 1 if (TILES - 1) % 2 == i else 0))

        def onehot_of(g):
            return onehot_0 if g == 0 else onehot[:, :, :]

        block = ctx.enter_context(nc.Block())

        @block.sync
        def _(sp):
            def load_x(g, half):
                if g >= 2:
                    wait_x_lo(sp, g - 1, half)
                n = samples_of(g)
                at = tiles_of(g)[0] * P * KC + half * XH * n
                sp.dma_start(x_raw[:, half, 0:XH * n], x_t[:, at:at + XH * n]).then_inc(x_loaded[half], 16)

            def stage_free(n):
                if n >= WSLOTS:
                    wait_staged_lo(sp, n - WSLOTS)

            def load_w(k):
                n = W0 + k
                stage_free(n)
                sp.dma_start(staging[:, n % WSLOTS, :], w_t[:, k, :]).then_inc(staged[n % WSLOTS], 16)

            sp.dma_start(idx_i[:, :], idx).then_inc(idx_loaded, 16)
            sp.dma_start(staging[:, X0 % WSLOTS, 0:KC * SHORT * P],
                         x_t[:, 0:KC * SHORT * P]).then_inc(staged[X0 % WSLOTS], 16)
            sp.dma_start(a_raw[:, :, :], a_t).then_inc(a_loaded, 16)
            load_w(0)
            load_x(1, 0)
            load_w(1)
            load_w(2)
            load_x(1, 1)
            for k in range(3, KC):
                load_w(k)
            stage_free(LAST)
            for part in range(3):
                for tab in range(TABLES):
                    at = (part * TABLES + tab) * R
                    sp.dma_start(last_raw[at:at + R, :],
                                 table[(tab + 1) * ROWS - 1, :].rearrange("(r o) -> r o", r=R)).then_inc(last_loaded, 16)
            stage_free(COMMON)
            for at in (0, R, LO):
                sp.dma_start(common_raw[at:at + R, :], common_t).then_inc(common_loaded, 16)
            for at in (2 * R, LO + R):
                sp.dma_start(common_raw[at:at + 1, :], bias).then_inc(common_loaded, 16)
            load_x(2, 0)
            load_x(2, 1)
            for t in range(TILES):
                g, j = place_of(t)
                if g >= 1 and j == (1 if g == 1 else 0) and g + 2 < GROUPS:
                    load_x(g + 2, 0)
                    load_x(g + 2, 1)
                if t < TILES - 1:
                    sp.wait_ge(evacuated, t + 1)
                    sp.dma_start(out[t * P:(t + 1) * P, :], out_sb[:, t % 2, :]).then_inc(stored[t % 2], 16)
                else:
                    for half in range(HALVES):
                        o = slice(half * BANK, (half + 1) * BANK)
                        sp.wait_ge(evacuated, t + 1 + half)
                        sp.dma_start(out[t * P:(t + 1) * P, o], out_sb[:, t % 2, o]).then_inc(stored[t % 2], 16)
            for i in range(2):
                sp.wait_ge(stored[i], stores(i))

        @block.gpsimd
        def _(pool):
            pool.memset(ones, 1.0).then_inc(ones_made, 1)
            pool.memset(in_mask[:, 0:PAD], 0.0).then_inc(consts_ready, 1)
            pool.memset(counts[:, :, :], 0.0).then_inc(consts_ready, 1)
            pool.memset(first[:, 1:GROUPS, 0:1], 0.0).then_inc(consts_ready, 1)
            pool.memset(first[:, 0:1, 0:1], float(P - PLACES)).then_inc(consts_ready, 1)
            pool.iota(count_f[:, :], pattern=[[1, GS]], base=1, channel_multiplier=0,
                      allow_small_or_imprecise_dtypes=True).then_inc(consts_ready, 1)
            pool.iota(chunk_no[:, :], pattern=[[1, CHUNKS]], base=-CHUNKS, channel_multiplier=0,
                      allow_small_or_imprecise_dtypes=True).then_inc(consts_ready, 1)
            pool.iota(count_0[:, :], pattern=[[0, COPIES], [1, PLACES]], base=P - PLACES + 1, channel_multiplier=0,
                      allow_small_or_imprecise_dtypes=True).then_inc(consts_ready, 1)
            pool.iota(half_no[:, :], pattern=[[1, CHUNKS // COPIES]], base=-CHUNKS, channel_multiplier=0,
                      allow_small_or_imprecise_dtypes=True).then_inc(consts_ready, 1)
            pool.iota(sample[:, 0:SHORT], pattern=[[P, SHORT]], base=1, channel_multiplier=1,
                      allow_small_or_imprecise_dtypes=True).then_inc(consts_ready, 1)
            pool.iota(sample[:, SHORT:TILES], pattern=[[0, GROUPS - 1], [P, GT]], base=1, channel_multiplier=1,
                      allow_small_or_imprecise_dtypes=True).then_inc(consts_ready, 1)
            pool.wait_ge(ones_made, 1)
            pool.affine_select(out=below, in_=ones, compare_op=ALU.is_gt, fill=0.0, base=0,
                               pattern=[[1, P]], channel_multiplier=-1).then_inc(consts_ready, 1)
            pool.affine_select(out=ident[:, :], in_=ones, compare_op=ALU.is_equal, fill=0.0, base=0,
                               pattern=[[1, P]], channel_multiplier=-1).then_inc(consts_ready, 1)
            pool.wait_ge(consts_ready, CONSTS - 1)
            pool.iota(half_no[PLACES:P, :], pattern=[[1, CHUNKS // COPIES]], base=CHUNKS // COPIES - CHUNKS,
                      channel_multiplier=0, allow_small_or_imprecise_dtypes=True).then_inc(consts_ready, 1)
            pool.wait_ge(consts_ready, CONSTS)
            for s in range(1, SLOTS):
                pool.memset(rows[:, s, :], 0.0).then_inc(rows_cleared[1], 1)

            def gather(g, chunks):
                pool.wait_ge(fetch_ready, g + 1)
                for c in chunks:
                    n = chunks_before(g) + c
                    if n >= SLOTS:
                        pool.wait_ge(rows_used, n - SLOTS + 1)
                    pool.indirect_dma_start(
                        out=rows[:, n % SLOTS, :], out_offset=None, in_=table_chunks,
                        in_offset=bass.IndirectOffsetOnAxis(ap=fetch[:, g % 2, c:c + 1], axis=0),
                        bounds_check=TABLE_CHUNKS - 1, oob_is_err=False).then_inc(gathered[n % SLOTS], 16)

            make_staged_lo(pool, W0)
            pool.memset(common_w[:, :].bitcast(f32), 0.0).then_inc(common_cleared, 1)
            pool.memset(low[:, :, NL:NL + NC], 0.0).then_inc(common_cleared, 1)
            pool.wait_ge(common_cleared, 2)
            for bias_row in (2 * R, LO + R):
                pool.memset(low[:, :, NL + bias_row:NL + bias_row + 1], 1.0).then_inc(common_cleared, 1)
            pool.wait_ge(rows_cleared[0], 1)
            pool.wait_ge(rows_cleared[1], SLOTS - 1)
            gather(0, range(0, SLOTS))
            make_x_lo(pool, 1, 1)
            make_staged_lo(pool, W0 + 3)
            gather(0, range(SLOTS, chunks_of(0)))
            gather(1, range(0, 2))
            make_staged_lo(pool, W0 + 5)
            gather(1, range(2, 3))
            make_staged_lo(pool, W0 + 6)
            gather(1, range(3, 4))
            make_staged_lo(pool, W0 + 7)
            gather(1, range(4, 6))
            make_x_lo(pool, 2, 1)
            gather(1, range(6, CHUNKS))
            for g in range(2, GROUPS):
                gather(g, range(0, 4 if g == 2 else 5))
                if g + 1 < GROUPS:
                    make_x_lo(pool, g + 1, 1)
                gather(g, range(4 if g == 2 else 5, CHUNKS))

            pool.wait_ge(longest_ready, 1)
            for i in range(2):
                pool.wait_ge(stored[i], stores(i))
            last_chunk = pool.to_reg(TABLE_CHUNKS - 1)
            with pool.If(pool.value_load(longest_i[0:1, 0:1], min_val=0, max_val=GC * P) > P):
                pool.sem_inc(over_turn, 1)
                with pool.Fori(0, TILES) as t:
                    pool.wait_ge(over_ready, t + 1)
                    pool.sem_inc(over_cleared, 1)
                    for n in range(TABLES * CHUNKS):
                        if n >= 2:
                            pool.wait_ge(over_used, t * (TABLES * CHUNKS) + n - 1)
                            pool.sem_inc(over_cleared, 1)
                        pool.indirect_dma_start(
                            out=rows[:, n % 2, :], out_offset=None, in_=table_chunks,
                            in_offset=bass.IndirectOffsetOnAxis(
                                ap=over_fetch[:, n // CHUNKS, n % CHUNKS:n % CHUNKS + 1], axis=0),
                            bounds_check=last_chunk, oob_is_err=False).then_inc(over_gathered[n % 2], 16)
                    pool.wait_ge(over_used, (t + 1) * (TABLES * CHUNKS))
                    pool.sem_inc(over_cleared, 1)
                    pool.dma_start(out[bass.ds(t * P, P), :], acc, accum_op=ALU.add).then_inc(over_stored, 16)
                    pool.wait_ge(over_stored, t * 16 + 16)
                    pool.sem_inc(over_turn, 1)

        @block.scalar
        def _(act):
            def make_x_hi(g, half):
                act.wait_ge(x_loaded[half], 16 * g)
                if g >= 2:
                    act.wait_ge(x_used, g - 1)
                act.activation(x_half(x_hi, g, half), x_raw_half(g, half), ACT.Copy).then_inc(x_hi_done, 1)

            def make_staged_hi(n):
                act.wait_ge(staged[n % WSLOTS], 16 * (n // WSLOTS + 1))
                hi, raw = ((x_hi[:, 0, :, 0:SHORT * P], x0_raw) if n == X0 else
                           (w_hi[:, n - W0, :], staging[:, n % WSLOTS, :]))
                act.activation(hi, raw, ACT.Copy).then_inc(staged_hi, 1)

            def copy_at(g):
                act.wait_ge(at_done, g + 1)
                if g >= 1:
                    act.wait_ge(a_done, g)
                n = samples_of(g)
                act.activation(at_sb[:, 0:n], at_ps[:, 0:n], ACT.Copy).then_inc(at_copied, 1)

            def spread_a(g):
                act.wait_ge(a_split_ready, 2 * (g + 1))
                ts, n = tiles_of(g), len(tiles_of(g))
                split = a_split[:, 0:n, :, :].rearrange("p t s r -> p t (s r)")
                act.activation(info[:, ts[0]:ts[-1] + 1, :, 2:INFO],
                               split.unsqueeze(2).broadcast_to([P, n, TABLES, 2 * R]), ACT.Copy).then_inc(info_ready, 1)
                if g == 0:
                    act.wait_ge(common_cleared, 4)
                else:
                    act.wait_ge(low_t_done, g)
                act.activation(low[:, 0:n, NL:NL + 2 * R], split, ACT.Copy).then_inc(common_spread, 1)
                act.activation(low[:, 0:n, NL + LO:NL + LO + R], a_split[:, 0:n, 0, :], ACT.Copy).then_inc(common_spread, 1)

            def copy_low(g):
                act.wait_ge(low_t_done, g + 1)
                if g >= 2:
                    act.wait_ge(tile_done, tiles_of(g - 1)[0])
                n = samples_of(g)
                act.activation(last_t[:, g % 2, 0:n], last_ps[:, 0:n], ACT.Copy).then_inc(low_copied, 1)
                act.activation(common_a[:, g % 2, 0:n], common_ps[:, 0:n], ACT.Copy).then_inc(low_copied, 1)

            def make_acc_hi(g):
                act.wait_ge(rows_used, chunks_before(g + 1))
                if g >= 1:
                    act.wait_ge(tile_done, tiles_of(g)[0])
                act.activation(acc_hi[:, :], acc, ACT.Copy).then_inc(acc_hi_done, 1)

            def evacuate(t):
                act.wait_ge(tile_done, t + 1)
                if t >= 2:
                    act.wait_ge(stored[t % 2], 16 * (t // 2))
                if t < TILES - 1:
                    act.activation(out_sb[:, t % 2, :], main_ps[t % GT][:, :], ACT.Copy).then_inc(evacuated, 1)
                else:
                    for half in range(HALVES):
                        o = slice(half * BANK, (half + 1) * BANK)
                        act.wait_ge(tile_done, t + 1 + half)
                        act.activation(out_sb[:, t % 2, o], main_ps[t % GT][:, o], ACT.Copy).then_inc(evacuated, 1)

            make_staged_hi(X0)
            act.wait_ge(a_loaded, 16)
            act.activation(a_hl[:, :, 0:R], a_raw[:, :, :], ACT.Copy, scale=2.0).then_inc(a_hi_done, 1)
            make_staged_hi(W0)
            make_x_hi(1, 0)
            copy_at(0)
            make_staged_hi(W0 + 1)
            make_staged_hi(W0 + 2)
            spread_a(0)
            make_x_hi(1, 1)
            make_staged_hi(W0 + 3)
            copy_low(0)
            make_staged_hi(W0 + 4)
            copy_at(1)
            make_staged_hi(W0 + 5)
            spread_a(1)
            make_staged_hi(W0 + 6)
            make_acc_hi(0)
            copy_low(1)
            make_staged_hi(W0 + 7)
            act.wait_ge(last_loaded, 16 * 3 * TABLES)
            act.activation(last_w[:, :], last_raw, ACT.Copy).then_inc(shared_hi, 1)
            act.wait_ge(common_loaded, 16 * 5)
            act.activation(common_w[0:CH, :], common_raw[0:CH, :], ACT.Copy).then_inc(shared_hi, 1)
            act.activation(common_w[LO:NC, :], common_raw[LO:NC, :], ACT.Copy).then_inc(shared_hi, 1)
            make_x_hi(2, 0)
            make_x_hi(2, 1)
            evacuate(0)
            copy_at(2)
            make_acc_hi(1)
            evacuate(1)
            spread_a(2)
            make_x_hi(3, 0)
            make_x_hi(3, 1)
            evacuate(2)
            copy_low(2)
            evacuate(3)
            copy_at(3)
            spread_a(3)
            make_acc_hi(2)
            evacuate(4)
            copy_low(3)
            for g in range(3, GROUPS):
                t, more = tiles_of(g)[0], g + 1 < GROUPS
                if more:
                    make_x_hi(g + 1, 0)
                    make_x_hi(g + 1, 1)
                evacuate(t - 2)
                if more:
                    copy_at(g + 1)
                    spread_a(g + 1)
                evacuate(t - 1)
                make_acc_hi(g)
                if more:
                    copy_low(g + 1)
                evacuate(t)
            evacuate(TILES - 2)
            evacuate(TILES - 1)

        @block.vector
        def _(dve):
            steps = [0]

            def link(ins):
                steps[0] += 1
                ins.then_inc(dve_step, 1)
                dve.wait_ge(dve_step, steps[0])

            def take_a(g):
                ts, n = tiles_of(g), len(tiles_of(g))
                t0, t1 = ts[0], ts[-1] + 1
                dve.wait_ge(a_done, g + 1)
                link(dve.tensor_copy(a_part[:, 0:n, :], a_ps[:, 0:n, 0:R]))
                dve.tensor_tensor(a_all[:, t0:t1, :], a_part[:, 0:n, :], a_ps[:, 0:n, R:2 * R],
                                  ALU.add).then_inc(a_taken, 1)
                dve.wait_ge(a_taken, g + 1)
                if g >= 1:
                    dve.wait_ge(common_spread, 2 * g)
                dve.tensor_copy(a_split[:, 0:n, 0, :].bitcast(f32r), a_all[:, t0:t1, :]).then_inc(a_split_ready, 1)
                dve.wait_ge(a_split_ready, 2 * g + 1)
                dve.tensor_tensor(a_split[:, 0:n, 1, :].bitcast(f32r), a_all[:, t0:t1, :], a_split[:, 0:n, 0, :],
                                  ALU.subtract).then_inc(a_split_ready, 1)
                dve.wait_ge(a_split_ready, 2 * (g + 1))
                if g >= 1:
                    dve.wait_ge(low_t_done, g)
                both = [P, n, TABLES, R]
                mask = last_mask[:, t0 * TABLES:t1 * TABLES].rearrange("p (t u) -> p t u", u=TABLES)
                mask = mask.unsqueeze(3).broadcast_to(both)
                for part, which in enumerate((0, 1, 0)):
                    masked = low[:, 0:n, part * TABLES * R:(part + 1) * TABLES * R]
                    dve.tensor_tensor(masked.rearrange("p t (u r) -> p t u r", u=TABLES),
                                      a_split[:, 0:n, which, :].unsqueeze(2).broadcast_to(both), mask,
                                      ALU.mult).then_inc(low_ready, 1)

            def make_onehot(g):
                if g >= 2:
                    dve.wait_ge(entry_a_done, g)
                n = len(tiles_of(g)) * TABLES
                number = count_0 if g == 0 else count_f
                dve.tensor_tensor(onehot_of(g), number[:, 0:P].unsqueeze(1).broadcast_to([P, n, P]),
                                  place[:, (g + 1) * GC - n:(g + 1) * GC].unsqueeze(2).broadcast_to([P, n, P]),
                                  ALU.is_equal).then_inc(onehot_ready, 1)

            def take_rows(g):
                dve.wait_ge(entry_row_done, g + 1)
                dve.tensor_copy(entry_row[:, :], entry_row_ps).then_inc(entry_row_taken, 1)
                dve.wait_ge(entry_row_taken, g + 1)
                link(dve.tensor_copy(entry_sample[:, g:g + 1], entry_row[:, 0:1]))
                link(dve.tensor_scalar(first_chunk[:, :], entry_row[:, 1:2], 0.0, ABSENT, ALU.is_equal, ALU.mult))
                link(dve.tensor_scalar(first_chunk[:, :], first_chunk[:, :], entry_row[:, 1:2], float(CHUNKS),
                                       ALU.add, ALU.mult))
                dve.tensor_scalar(fetch[:, g % 2, 0:chunks_of(g)], (half_no if g == 0 else chunk_no)[:, :],
                                  first_chunk[:, 0:1], None, ALU.add).then_inc(fetch_ready, 1)

            def take_entries(g):
                dve.wait_ge(entry_a_done, g + 1)
                dve.tensor_copy(entry_a[:, :], entry_a_ps).then_inc(entry_a_taken, 1)
                dve.wait_ge(entry_a_taken, g + 1)
                if g == 0:
                    n = R // COPIES
                    for copy in range(COPIES):
                        on = slice(copy * PLACES, (copy + 1) * PLACES)
                        link(dve.tensor_tensor(a_entry[on, 0:n], entry_a[on, copy * n:(copy + 1) * n],
                                               entry_a[on, R + copy * n:R + (copy + 1) * n], ALU.add))
                else:
                    link(dve.tensor_tensor(a_entry[:, :], entry_a[:, 0:R], entry_a[:, R:2 * R], ALU.add))
                if g >= 2:
                    dve.wait_ge(tile_done, tiles_of(g - 1)[0])
                n = samples_of(g)
                dve.tensor_scalar(select[:, g % 2, 0:n], count_f[:, 0:n], entry_sample[:, g:g + 1], None,
                                  ALU.is_equal).then_inc(select_ready, 1)

            def multiply_rows(rows_r, a_r, start):
                if start:
                    return dve.tensor_scalar(acc, rows_r, a_r, None, ALU.mult)
                return dve.scalar_tensor_tensor(acc, rows_r, a_r, acc, ALU.mult, ALU.add)

            def row_products(g, chunks):
                for c in chunks:
                    n = chunks_before(g) + c
                    dve.wait_ge(gathered[n % SLOTS], 16 * (n // SLOTS + 1))
                    for j in range(RB):
                        r = c * RB + j
                        ins = multiply_rows(rows[:, n % SLOTS, j * OUT_F:(j + 1) * OUT_F], a_entry[:, r:r + 1], r == 0)
                        if j < RB - 1:
                            link(ins)
                    ins.then_inc(rows_used, 1)
                    dve.wait_ge(rows_used, n + 1)

            def make_acc_lo(g):
                if g >= 1:
                    dve.wait_ge(tile_done, tiles_of(g)[0])
                dve.wait_ge(acc_hi_done, g + 1)
                dve.tensor_tensor(acc_lo[:, :], acc, acc_hi[:, :].bitcast(f32), ALU.subtract).then_inc(acc_lo_done, 1)
                dve.wait_ge(acc_lo_done, g + 1)

            dve.memset(rows[:, 0, :], 0.0).then_inc(rows_cleared[0], 1)
            dve.wait_ge(idx_loaded, 16)
            link(dve.tensor_copy(row[:, :], idx_i[:, :]))
            link(dve.tensor_scalar(wrap[:, :], row[:, :], 0.0, float(ROWS), ALU.is_lt, ALU.mult))
            link(dve.tensor_tensor(row[:, :], row[:, :], wrap[:, :], ALU.add))
            link(dve.tensor_scalar(row[:, :], row[:, :], 0.0, float(ROWS - 1), ALU.max, ALU.min))
            dve.wait_ge(consts_ready, CONSTS)
            dve.tensor_scalar(in_mask[:, PAD:PAD + COLS], row[:, :], float(ROWS - 1), None,
                              ALU.is_lt).then_inc(in_mask_ready, 1)
            link(dve.tensor_scalar(last_mask[:, :], row[:, :], float(ROWS - 1), None, ALU.is_ge))
            row_v = row[:, :].rearrange("p (t u) -> p t u", u=TABLES)
            for tab in range(TABLES):
                link(dve.tensor_scalar(row_v[:, :, tab], row_v[:, :, tab], float(tab * ROWS + 1), None, ALU.add))
            link(dve.tensor_copy(info[:, :, :, 1], row_v))
            link(dve.tensor_copy(info[:, :, :, 0], sample[:, :].unsqueeze(2).broadcast_to([P, TILES, TABLES])))
            make_staged_lo(dve, X0)
            dve.wait_ge(a_hi_done, 1)
            dve.scalar_tensor_tensor(a_hl[:, :, R:2 * R], a_raw[:, :, :], 2.0, a_hl[:, :, 0:R].bitcast(f32),
                                     ALU.mult, ALU.subtract).then_inc(a_lo_done, 1)
            dve.wait_ge(counts_done, 1)
            dve.tensor_copy(counts[:, :, PAD:PAD + COLS],
                            counts_ps.rearrange("p (s c) -> p s c", s=2)).then_inc(counts_taken, 1)
            dve.wait_ge(counts_taken, 1)
            total = counts[:, 1, :].rearrange("p (g j) -> p g j", j=GC)
            for j in range(GC):
                link(dve.tensor_tensor(first[:, :, j + 1], first[:, :, j], total[:, :, j], ALU.add))
            place_v = place[:, :].rearrange("p (g j) -> p g j", j=GC)
            link(dve.tensor_tensor(place_v, counts[:, 0, :].rearrange("p (g j) -> p g j", j=GC),
                                   first[:, :, 0:GC], ALU.add))
            dve.wait_ge(in_mask_ready, 1)
            link(dve.scalar_tensor_tensor(place[:, :], place[:, :], 1.0, in_mask[:, :], ALU.add, ALU.mult))
            make_onehot(0)
            take_rows(0)
            take_a(0)
            make_x_lo(dve, 1, 0)
            make_onehot(1)
            take_entries(0)
            make_staged_lo(dve, W0 + 1)
            make_staged_lo(dve, W0 + 2)
            row_products(0, range(0, 1))
            take_rows(1)
            row_products(0, range(1, 3))
            make_staged_lo(dve, W0 + 4)
            take_a(1)
            row_products(0, range(3, 4))
            take_entries(1)
            make_acc_lo(0)
            make_onehot(2)
            row_products(1, range(0, 2))
            dve.wait_ge(shared_hi, 3)
            dve.tensor_tensor(last_w[LO:NL, :], last_raw[LO:NL, :], last_w[LO:NL, :].bitcast(f32),
                              ALU.subtract).then_inc(shared_ready, 1)
            dve.tensor_tensor(common_w[LO:NC, :], common_raw[LO:NC, :], common_w[LO:NC, :].bitcast(f32),
                              ALU.subtract).then_inc(shared_ready, 1)
            row_products(1, range(2, 4))
            make_x_lo(dve, 2, 0)
            take_rows(2)
            row_products(1, range(4, CHUNKS))
            make_acc_lo(1)
            take_a(2)
            take_entries(2)
            for g in range(2, GROUPS):
                more, early = g + 1 < GROUPS, 3 if g == 2 else 5
                if more:
                    make_onehot(g + 1)
                row_products(g, range(0, early))
                if more:
                    take_rows(g + 1)
                    make_x_lo(dve, g + 1, 0)
                row_products(g, range(early, CHUNKS))
                if more:
                    take_a(g + 1)
                make_acc_lo(g)
                if more:
                    take_entries(g + 1)

            link(dve.tensor_reduce(longest[:, :], first[:, :, GC], axis=AX.X, op=ALU.max))
            dve.tensor_copy(longest_i[:, :], longest[:, :]).then_inc(longest_ready, 1)
            dve.wait_ge(longest_ready, 1)
            with dve.If(dve.value_load(longest_i[0:1, 0:1], min_val=0, max_val=GC * P) > P):
                link(dve.tensor_scalar(over[:, :], place[:, PAD:PAD + COLS], float(P), None, ALU.is_gt))
                link(dve.tensor_scalar(over_chunk[:, :], over[:, :], -ABSENT, ABSENT, ALU.mult, ALU.add))
                link(dve.tensor_tensor(over_chunk[:, :], over_chunk[:, :], row[:, :], ALU.add))
                link(dve.tensor_scalar(over_chunk[:, :], over_chunk[:, :], float(CHUNKS), None, ALU.mult))
                link(dve.tensor_tensor(over_fetch_all[:, :, :],
                                       over_chunk[:, :].unsqueeze(2).broadcast_to([P, COLS, CHUNKS]),
                                       chunk_no[:, :].unsqueeze(1).broadcast_to([P, COLS, CHUNKS]), ALU.add))
                with dve.Fori(0, TILES) as t:
                    before = steps[0]
                    per_turn = TABLES + TABLES * (R - CHUNKS)

                    def turn_link(ins, n):
                        ins.then_inc(dve_step, 1)
                        dve.wait_ge(dve_step, t * per_turn + (before + n))

                    dve.wait_ge(over_turn, t + 1)
                    for tab in range(TABLES):
                        turn_link(dve.tensor_scalar(over_a[:, tab, :], a_all[:, bass.ds(t, 1), :].squeeze(1),
                                                    over[:, bass.ds(t * TABLES + tab, 1)], None, ALU.mult), tab + 1)
                    dve.tensor_copy(over_fetch[:, :, :],
                                    over_fetch_all[:, bass.ds(t * TABLES, TABLES), :]).then_inc(over_ready, 1)
                    links = TABLES
                    for n in range(TABLES * CHUNKS):
                        tab, c = divmod(n, CHUNKS)
                        dve.wait_ge(over_gathered[n % 2], t * (16 * TABLES * CHUNKS // 2) + 16 * (n // 2 + 1))
                        for j in range(RB):
                            r = c * RB + j
                            ins = multiply_rows(rows[:, n % 2, j * OUT_F:(j + 1) * OUT_F], over_a[:, tab, r:r + 1],
                                                n == 0 and j == 0)
                            if j < RB - 1:
                                links += 1
                                turn_link(ins, links)
                        ins.then_inc(over_used, 1)
                        dve.wait_ge(over_used, t * (TABLES * CHUNKS) + n + 1)

        @block.tensor
        def _(pe):
            def rank_a(g):
                wait_x_lo(pe, g, 0)
                wait_x_lo(pe, g, 1)
                if g >= 1:
                    pe.wait_ge(entry_row_taken, g + 1)
                    pe.wait_ge(low_copied, 2 * g)
                n = samples_of(g)
                for k in range(KC):
                    pe.matmul(at_ps[:, 0:n], a_hl[:, k, :], x_hi[:, g % 2, k, 0:n], start=(k == 0), stop=False)
                    last = pe.matmul(at_ps[0:R, 0:n], a_hl[:, k, 0:R], x_lo[:, g % 2, k, 0:n], start=False,
                                     stop=(k == KC - 1))
                last.then_inc(at_done, 1)

            def transpose_a(g):
                pe.wait_ge(at_copied, g + 1)
                if g == 0:
                    pe.wait_ge(counts_taken, 1)
                else:
                    pe.wait_ge(low_copied, 2 * g)
                for j in range(len(tiles_of(g))):
                    last = pe.transpose(a_ps[:, j, :], at_sb[:, j * P:(j + 1) * P], ident[0:2 * R, 0:2 * R])
                last.then_inc(a_done, 1)

            def pack_rows(g):
                pe.wait_ge(onehot_ready, g + 1)
                if g == 0:
                    pe.wait_ge(at_copied, 1)
                elif g == 1:
                    pe.wait_ge(entry_a_taken, g)
                elif g >= 2:
                    pe.wait_ge(low_copied, 2 * g)
                cols = [(t, tab) for t in tiles_of(g) for tab in range(TABLES)]
                for c, (t, tab) in enumerate(cols):
                    last = pe.matmul(entry_row_ps, onehot_of(g)[:, c, :], info[:, t, tab, 0:2], start=(c == 0),
                                     stop=(c == len(cols) - 1))
                last.then_inc(entry_row_done, 1)

            def pack_a(g):
                pe.wait_ge(info_ready, g + 1)
                if g == 0:
                    pe.wait_ge(entry_row_taken, 1)
                else:
                    pe.wait_ge(at_copied, g + 1)
                cols = [(t, tab) for t in tiles_of(g) for tab in range(TABLES)]
                for c, (t, tab) in enumerate(cols):
                    last = pe.matmul(entry_a_ps, onehot_of(g)[:, c, :], info[:, t, tab, 2:INFO], start=(c == 0),
                                     stop=(c == len(cols) - 1))
                last.then_inc(entry_a_done, 1)

            def transpose_low(g):
                pe.wait_ge(low_ready, 3 * (g + 1))
                pe.wait_ge(common_spread, 2 * (g + 1))
                pe.wait_ge(entry_a_taken, g + 1)
                pe.wait_ge(entry_row_taken, max(g + 1, 2))
                for j in range(len(tiles_of(g))):
                    to = slice(j * P, (j + 1) * P)
                    pe.transpose(last_ps[:, to], low[:, j, 0:NL], ident[:, :])
                    last = pe.transpose(common_ps[:, to], low[:, j, NL:NL + NC], ident[:, :])
                last.then_inc(low_t_done, 1)

            def base_step(t, half, k):
                g, j = place_of(t)
                to = main_ps[t % GT][:, half * BANK:(half + 1) * BANK]
                b, o = slice(j * P, (j + 1) * P), slice(half * BANK, (half + 1) * BANK)
                pe.matmul(to, x_hi[:, g % 2, k, b], w_hi[:, k, o], start=(k == 0), stop=False)
                pe.matmul(to, x_hi[:, g % 2, k, b], w_lo[:, k, o], start=False, stop=False)
                return pe.matmul(to, x_lo[:, g % 2, k, b], w_hi[:, k, o], start=False, stop=False)

            def base(t, half, chunks=range(KC)):
                g, _ = place_of(t)
                wait_x_lo(pe, g, 0)
                wait_x_lo(pe, g, 1)
                pe.wait_ge(evacuated, t - GT + 1)
                for k in chunks:
                    last = base_step(t, half, k)
                if t == tiles_of(g)[-1] and half == HALVES - 1 and k == KC - 1:
                    last.then_inc(x_used, 1)

            def finish(t, halves=range(HALVES)):
                g, j = place_of(t)
                b = slice(j * P, (j + 1) * P)
                pe.wait_ge(shared_ready, 2)
                pe.wait_ge(low_copied, 2 * (g + 1))
                for half in halves:
                    o = slice(half * BANK, (half + 1) * BANK)
                    pe.matmul(main_ps[t % GT][:, o], last_t[:, g % 2, b], last_w[:, o], start=False, stop=False)
                    pe.matmul(main_ps[t % GT][:, o], common_a[:, g % 2, b], common_w[:, o], start=False, stop=False)
                pe.wait_ge(select_ready, g + 1)
                pe.wait_ge(acc_lo_done, g + 1)
                for half in halves:
                    o = slice(half * BANK, (half + 1) * BANK)
                    pe.matmul(main_ps[t % GT][:, o], select[:, g % 2, b], acc_hi[:, o], start=False, stop=False)
                    last = pe.matmul(main_ps[t % GT][:, o], select[:, g % 2, b], acc_lo[:, o], start=False, stop=True)
                last.then_inc(tile_done, 1)

            pe.wait_ge(consts_ready, CONSTS)
            pe.wait_ge(ones_made, 1)
            pe.wait_ge(in_mask_ready, 1)
            pe.matmul(counts_ps[:, 0:COLS], below, in_mask[:, PAD:PAD + COLS], start=True, stop=True)
            pe.matmul(counts_ps[:, COLS:2 * COLS], ones, in_mask[:, PAD:PAD + COLS], start=True,
                      stop=True).then_inc(counts_done, 1)
            def first_tiles(k, tiles):
                wait_staged_lo(pe, W0 + k)
                for t in tiles:
                    g, _ = place_of(t)
                    wait_x_lo(pe, g, k // XH)
                    for half in range(HALVES):
                        last = base_step(t, half, k)
                    if g == 0 and k == KC - 1:
                        last.then_inc(x_used, 1)

            pe.wait_ge(a_lo_done, 1)
            rank_a(0)
            pack_rows(0)
            transpose_a(0)
            first_tiles(0, range(0, 1))
            pack_a(0)
            first_tiles(0, range(1, 3))
            pack_rows(1)
            first_tiles(1, range(0, 2))
            transpose_low(0)
            first_tiles(1, range(2, 3))
            rank_a(1)
            first_tiles(2, range(0, 1))
            transpose_a(1)
            first_tiles(2, range(1, 3))
            pack_a(1)
            first_tiles(3, range(0, 3))
            first_tiles(4, range(0, 1))
            transpose_low(1)
            first_tiles(4, range(1, 3))
            first_tiles(5, range(0, 3))
            first_tiles(6, range(0, 3))
            first_tiles(7, range(0, 1))
            finish(0)
            first_tiles(7, range(1, 3))
            pack_rows(2)
            base(3, 0)
            base(3, 1)
            rank_a(2)
            transpose_a(2)
            finish(1)
            base(4, 0, range(0, KC // 2))
            pack_a(2)
            base(4, 0, range(KC // 2, KC))
            finish(2)
            transpose_low(2)
            base(4, 1, range(0, KC // 2))
            pack_rows(3)
            base(4, 1, range(KC // 2, KC))
            base(5, 0)
            finish(3)
            rank_a(3)
            base(5, 1)
            transpose_a(3)
            base(6, 0)
            finish(4)
            pack_a(3)
            base(6, 1)
            transpose_low(3)
            for g in range(3, GROUPS):
                t, more = tiles_of(g)[0], g + 1 < GROUPS
                base(t, 0)
                finish(t - 2)
                base(t, 1, range(0, KC // 2))
                if more:
                    pack_rows(g + 1)
                base(t, 1, range(KC // 2, KC))
                base(t + 1, 0, range(0, KC // 2))
                if more:
                    rank_a(g + 1)
                base(t + 1, 0, range(KC // 2, KC))
                if more:
                    transpose_a(g + 1)
                finish(t - 1)
                base(t + 1, 1, range(0, KC // 2))
                if more:
                    pack_a(g + 1)
                base(t + 1, 1, range(KC // 2, KC))
                if more:
                    transpose_low(g + 1)
                base(t + 2, 0)
                finish(t)
                if not more:
                    finish(t + 1)
                    finish(t + 2, range(0, 1))
                base(t + 2, 1)
            finish(TILES - 1, range(1, HALVES))


def kernel(**inputs):
    import numpy as np
    import concourse.bacc as bacc
    from concourse.bass_utils import run_bass_kernel_spmd

    a = {k: np.asarray(v) for k, v in inputs.items()}
    idx = np.stack([a["r_user_indices"].reshape(TILES, P), a["r_item_indices"].reshape(TILES, P)], axis=-1)
    x = a["r_x"].reshape(BATCH, KC, P).transpose(2, 1, 0)
    at = [tiles_of(g)[0] * P for g in range(GROUPS)]
    x_t = np.concatenate([x[:, :, at[g]:at[g] + samples_of(g)].reshape(P, -1) for g in range(GROUPS)], axis=1)
    tables = np.concatenate([a["L0_rec_B_user"], a["L0_rec_B_item"]], axis=0).transpose(0, 2, 1)
    arrays = {
        "idx": idx.transpose(1, 0, 2).reshape(P, COLS),
        "x_t": x_t,
        "w_t": a["L0_rec_W_base"].reshape(OUT_F, KC, P).transpose(2, 1, 0),
        "a_t": a["L0_rec_A"].reshape(R, KC, P).transpose(2, 1, 0),
        "bias": a["L0_rec_b_base"].reshape(1, OUT_F),
        "common_t": a["L0_rec_W_common"].T,
        "table": tables.reshape(TABLES * ROWS, R * OUT_F),
    }
    arrays = {k: np.ascontiguousarray(v) for k, v in arrays.items()}
    nc = bacc.Bacc("TRN2", target_bir_lowering=False, num_devices=1)
    args = [nc.dram_tensor(k, v.shape, mybir.dt.from_np(v.dtype), kind="ExternalInput").ap() for k, v in arrays.items()]
    args.append(nc.dram_tensor("out", (BATCH, OUT_F), mybir.dt.float32, kind="ExternalOutput").ap())
    rec_kernel(nc, *args)
    return run_bass_kernel_spmd(nc, [arrays], core_ids=[0]).results[0]["out"]
```
